# Optimizing a Trainium2 kernel written in Bass

```python
import numpy as np
import jax
import jax.numpy as jnp

def _softmax(x, axis=-1):
    return jax.nn.softmax(x, axis=axis)

def _gelu(x):
    return jax.nn.gelu(x, approximate=True)

def _silu(x):
    return jax.nn.silu(x)

def _sigmoid(x):
    return jax.nn.sigmoid(x)

def _layernorm(x, axis=-1, eps=1e-05):
    m = jnp.mean(x, axis=axis, keepdims=True)
    v = jnp.var(x, axis=axis, keepdims=True)
    return (x - m) / jnp.sqrt(v + eps)

def _scatter_add(tgt, idx, src, axis=0):
    return tgt.at[idx].add(src)

def _segment_sum(src, seg, n):
    return jax.ops.segment_sum(src, seg, n)
kernel_name = 'mk_conv_preact_d1_conv_nhwc768_r4_1a7e5a'

def setup_inputs(seed: int=0):
    np.random.seed(seed)
    _w = jnp.asarray

    def _rec_inputs():
        import jax
        import jax.numpy as jnp
        _gk = jax.random.key(seed)
        x = -0.0005963 + 1.001 * jax.random.normal(jax.random.fold_in(_gk, 1), (2, 16, 32, 192), jnp.float32)
        return x
    x = _rec_inputs()

    def _L0_conv_setup():
        import jax, jax.numpy as jnp
        import numpy as np
        D_MODEL = 192
        N_HEADS = 12
        HEAD_DIM = D_MODEL // N_HEADS
        FFN_DIM = 768
        MAX_WAVELENGTH = 10000.0
        ROPE_PERCENT = 0.5
        NORM_EPS = 1e-05

        def _layernorm(x, g, b):
            mu = jnp.mean(x, axis=-1, keepdims=True)
            var = jnp.mean(jnp.square(x - mu), axis=-1, keepdims=True)
            return (x - mu) * jax.lax.rsqrt(var + NORM_EPS) * g + b

        def _apply_p_rope(x, positions):
            half = HEAD_DIM // 2
            rope_angles = int(ROPE_PERCENT * HEAD_DIM) // 2
            fraction = 2.0 * jnp.arange(rope_angles, dtype=jnp.float32) / HEAD_DIM
            timescale = jnp.concatenate([MAX_WAVELENGTH ** fraction, jnp.full((half - rope_angles,), jnp.inf, dtype=jnp.float32)])
            angles = positions[:, None].astype(jnp.float32) / timescale[None, :]
            sin = jnp.sin(angles)[None, None]
            cos = jnp.cos(angles)[None, None]
            x1, x2 = jnp.split(x, 2, axis=-1)
            return jnp.concatenate([x1 * cos - x2 * sin, x2 * cos + x1 * sin], axis=-1)

        def _forward(hidden_state, wq, bq, wk, bk, wv, bv, wo, bo, attn_biases, ln1_g, ln1_b, ln3_g, ln3_b, w1, b1, w2, b2):
            B, C, S, D = hidden_state.shape
            T = C * S
            flat = hidden_state.reshape(B, T, D)
            ni = _layernorm(flat, ln1_g, ln1_b)
            scaling = HEAD_DIM ** (-0.5)
            q = (ni @ wq + bq) * scaling
            k = ni @ wk + bk
            v = ni @ wv + bv
            to_heads = lambda t: t.reshape(B, T, N_HEADS, HEAD_DIM).transpose(0, 2, 1, 3)
            q, k, v = (to_heads(q), to_heads(k), to_heads(v))
            positions = jnp.arange(T)
            k = _apply_p_rope(k, positions)
            q = _apply_p_rope(q, positions)
            scores = jnp.einsum('bhtd,bhsd->bhts', q, k)
            variate_ids = positions // S
            same = (variate_ids[:, None] == variate_ids[None, :]).astype(scores.dtype)
            variate_bias = same[None, :, :] * attn_biases[:, 0][:, None, None] + (1.0 - same[None, :, :]) * attn_biases[:, 1][:, None, None]
            scores = scores + variate_bias[None]
            probs = jax.nn.softmax(scores, axis=-1)
            attn = jnp.einsum('bhts,bhsd->bhtd', probs, v)
            attn = attn.transpose(0, 2, 1, 3).reshape(B, T, D)
            attn = attn @ wo + bo
            flat = flat + attn
            ff_in = _layernorm(flat, ln3_g, ln3_b)
            ff = jax.nn.gelu(ff_in @ w1 + b1, approximate=False) @ w2 + b2
            flat = flat + ff
            return flat.reshape(B, C, S, D)
        key = jax.random.key(seed)
        ks = jax.random.split(key, 12)
        B, C, S = (2, 16, 32)
        init = lambda k, shape: jax.random.normal(k, shape, dtype=jnp.float32) * 0.02
        return {'hidden_state': jax.random.normal(ks[0], (B, C, S, D_MODEL), dtype=jnp.float32), 'wq': init(ks[1], (D_MODEL, D_MODEL)), 'bq': jnp.zeros((D_MODEL,), jnp.float32), 'wk': init(ks[2], (D_MODEL, D_MODEL)), 'bk': jnp.zeros((D_MODEL,), jnp.float32), 'wv': init(ks[3], (D_MODEL, D_MODEL)), 'bv': jnp.zeros((D_MODEL,), jnp.float32), 'wo': init(ks[4], (D_MODEL, D_MODEL)), 'bo': jnp.zeros((D_MODEL,), jnp.float32), 'attn_biases': init(ks[5], (N_HEADS, 2)), 'ln1_g': jnp.ones((D_MODEL,), jnp.float32), 'ln1_b': jnp.zeros((D_MODEL,), jnp.float32), 'ln3_g': jnp.ones((D_MODEL,), jnp.float32), 'ln3_b': jnp.zeros((D_MODEL,), jnp.float32), 'w1': init(ks[6], (D_MODEL, FFN_DIM)), 'b1': jnp.zeros((FFN_DIM,), jnp.float32), 'w2': init(ks[7], (FFN_DIM, D_MODEL)), 'b2': jnp.zeros((D_MODEL,), jnp.float32)}
    _L0_conv_all = _L0_conv_setup()
    _L0_conv_in = {k: v for k, v in _L0_conv_all.items() if k in ('wq', 'bq', 'wk', 'bk', 'wv', 'bv', 'wo', 'bo', 'attn_biases', 'ln1_g', 'ln1_b', 'ln3_g', 'ln3_b', 'w1', 'b1', 'w2', 'b2')}
    del _L0_conv_all
    return {'x': x, 'L0_conv_wq': _L0_conv_in['wq'], 'L0_conv_bq': _L0_conv_in['bq'], 'L0_conv_wk': _L0_conv_in['wk'], 'L0_conv_bk': _L0_conv_in['bk'], 'L0_conv_wv': _L0_conv_in['wv'], 'L0_conv_bv': _L0_conv_in['bv'], 'L0_conv_wo': _L0_conv_in['wo'], 'L0_conv_bo': _L0_conv_in['bo'], 'L0_conv_attn_biases': _L0_conv_in['attn_biases'], 'L0_conv_ln1_g': _L0_conv_in['ln1_g'], 'L0_conv_ln1_b': _L0_conv_in['ln1_b'], 'L0_conv_ln3_g': _L0_conv_in['ln3_g'], 'L0_conv_ln3_b': _L0_conv_in['ln3_b'], 'L0_conv_w1': _L0_conv_in['w1'], 'L0_conv_b1': _L0_conv_in['b1'], 'L0_conv_w2': _L0_conv_in['w2'], 'L0_conv_b2': _L0_conv_in['b2']}

def reference(x, L0_conv_wq, L0_conv_bq, L0_conv_wk, L0_conv_bk, L0_conv_wv, L0_conv_bv, L0_conv_wo, L0_conv_bo, L0_conv_attn_biases, L0_conv_ln1_g, L0_conv_ln1_b, L0_conv_ln3_g, L0_conv_ln3_b, L0_conv_w1, L0_conv_b1, L0_conv_w2, L0_conv_b2):
    import jax
    import jax.numpy as jnp

    def _L0_conv_ref(hidden_state, wq, bq, wk, bk, wv, bv, wo, bo, attn_biases, ln1_g, ln1_b, ln3_g, ln3_b, w1, b1, w2, b2):
        import jax, jax.numpy as jnp
        import numpy as np
        D_MODEL = 192
        N_HEADS = 12
        HEAD_DIM = D_MODEL // N_HEADS
        FFN_DIM = 768
        MAX_WAVELENGTH = 10000.0
        ROPE_PERCENT = 0.5
        NORM_EPS = 1e-05

        def _layernorm(x, g, b):
            mu = jnp.mean(x, axis=-1, keepdims=True)
            var = jnp.mean(jnp.square(x - mu), axis=-1, keepdims=True)
            return (x - mu) * jax.lax.rsqrt(var + NORM_EPS) * g + b

        def _apply_p_rope(x, positions):
            half = HEAD_DIM // 2
            rope_angles = int(ROPE_PERCENT * HEAD_DIM) // 2
            fraction = 2.0 * jnp.arange(rope_angles, dtype=jnp.float32) / HEAD_DIM
            timescale = jnp.concatenate([MAX_WAVELENGTH ** fraction, jnp.full((half - rope_angles,), jnp.inf, dtype=jnp.float32)])
            angles = positions[:, None].astype(jnp.float32) / timescale[None, :]
            sin = jnp.sin(angles)[None, None]
            cos = jnp.cos(angles)[None, None]
            x1, x2 = jnp.split(x, 2, axis=-1)
            return jnp.concatenate([x1 * cos - x2 * sin, x2 * cos + x1 * sin], axis=-1)

        def _forward(hidden_state, wq, bq, wk, bk, wv, bv, wo, bo, attn_biases, ln1_g, ln1_b, ln3_g, ln3_b, w1, b1, w2, b2):
            B, C, S, D = hidden_state.shape
            T = C * S
            flat = hidden_state.reshape(B, T, D)
            ni = _layernorm(flat, ln1_g, ln1_b)
            scaling = HEAD_DIM ** (-0.5)
            q = (ni @ wq + bq) * scaling
            k = ni @ wk + bk
            v = ni @ wv + bv
            to_heads = lambda t: t.reshape(B, T, N_HEADS, HEAD_DIM).transpose(0, 2, 1, 3)
            q, k, v = (to_heads(q), to_heads(k), to_heads(v))
            positions = jnp.arange(T)
            k = _apply_p_rope(k, positions)
            q = _apply_p_rope(q, positions)
            scores = jnp.einsum('bhtd,bhsd->bhts', q, k)
            variate_ids = positions // S
            same = (variate_ids[:, None] == variate_ids[None, :]).astype(scores.dtype)
            variate_bias = same[None, :, :] * attn_biases[:, 0][:, None, None] + (1.0 - same[None, :, :]) * attn_biases[:, 1][:, None, None]
            scores = scores + variate_bias[None]
            probs = jax.nn.softmax(scores, axis=-1)
            attn = jnp.einsum('bhts,bhsd->bhtd', probs, v)
            attn = attn.transpose(0, 2, 1, 3).reshape(B, T, D)
            attn = attn @ wo + bo
            flat = flat + attn
            ff_in = _layernorm(flat, ln3_g, ln3_b)
            ff = jax.nn.gelu(ff_in @ w1 + b1, approximate=False) @ w2 + b2
            flat = flat + ff
            return flat.reshape(B, C, S, D)
        return _forward(hidden_state, wq, bq, wk, bk, wv, bv, wo, bo, attn_biases, ln1_g, ln1_b, ln3_g, ln3_b, w1, b1, w2, b2)

    def _gn(v, G=32, eps=1e-05):
        B_, H_, W_, C_ = v.shape
        g = v.reshape(B_, H_, W_, G, C_ // G)
        m = jnp.mean(g, axis=(1, 2, 4), keepdims=True)
        s = jnp.var(g, axis=(1, 2, 4), keepdims=True)
        return ((g - m) / jnp.sqrt(s + eps)).reshape(v.shape)

    def _ln_c(v, eps=1e-06):
        m = jnp.mean(v, axis=-1, keepdims=True)
        s = jnp.var(v, axis=-1, keepdims=True)
        return (v - m) / jnp.sqrt(s + eps)

    def _ln_t(v, eps=1e-05):
        m = jnp.mean(v, axis=-1, keepdims=True)
        s = jnp.var(v, axis=-1, keepdims=True)
        return (v - m) / jnp.sqrt(s + eps)

    def _to_tokens(v):
        B_, H_, W_, C_ = v.shape
        return v.reshape(B_, H_ * W_, C_)

    def _from_tokens(t, like):
        return t.reshape(like.shape)
    x = x + _L0_conv_ref(_gn(x), L0_conv_wq, L0_conv_bq, L0_conv_wk, L0_conv_bk, L0_conv_wv, L0_conv_bv, L0_conv_wo, L0_conv_bo, L0_conv_attn_biases, L0_conv_ln1_g, L0_conv_ln1_b, L0_conv_ln3_g, L0_conv_ln3_b, L0_conv_w1, L0_conv_b1, L0_conv_w2, L0_conv_b2)
    return x

_drawn_inputs = setup_inputs


def setup_inputs(seed=0):
    import zlib

    import numpy as np

    out = dict(_drawn_inputs(seed))
    spreads = {'L0_conv_bq': (0.0, 0.8),
     'L0_conv_bk': (0.0, 0.8),
     'L0_conv_bv': (0.0, 0.598),
     'L0_conv_bo': (0.0, 0.369),
     'L0_conv_ln1_g': (1.0, 0.6),
     'L0_conv_ln1_b': (0.0, 0.8),
     'L0_conv_ln3_g': (1.0, 0.6),
     'L0_conv_ln3_b': (0.0, 2.0),
     'L0_conv_b1': (0.0, 0.557),
     'L0_conv_b2': (0.0, 0.331)}
    factors = {'L0_conv_wq': 8.0,
     'L0_conv_wk': 8.0,
     'L0_conv_wv': 8.0,
     'L0_conv_wo': 3.995,
     'L0_conv_attn_biases': 42.727}
    for name, (base, spread) in spreads.items():
        noise = np.random.default_rng([zlib.crc32(name.encode()), seed]).standard_normal(out[name].shape)
        drawn = base * np.exp(spread * noise) if base else spread * noise
        out[name] = jnp.asarray(drawn.astype(out[name].dtype))
    for name, factor in factors.items():
        out[name] = (out[name] * factor).astype(out[name].dtype)
    return out
```

```python
import concourse.bass as bass
from concourse import mybir
from contextlib import ExitStack

fp32 = mybir.dt.float32
fp32r = mybir.dt.float32r
int32 = mybir.dt.int32
ALU = mybir.AluOpType
ACT = mybir.ActivationFunctionType
AX = mybir.AxisListType

P = 128
B, C, S, D = 2, 16, 32, 192
T = C * S
NT = T // P
NH, HD = 12, 16
F = 768
NF = F // P
GROUPS, GW = 32, D // 32
GJ = 4
NG = NH // GJ
EPS = 1e-5
KA, KB = P, D - P
DQK = 2 * D

ROW_BIAS, ROW_MAX, ROWS = 64, 98, 100
VW = 32

COL = {}
_at = 0
for _name, _n in (("ident", P), ("cos", NT * 4), ("sin", NT * 4), ("nsin", NT * 4), ("g1", 2), ("c1", 2),
                  ("g3", 2), ("c3", 2), ("b1", NF), ("low", 1), ("ca", 1), ("cb", 1), ("ab0", NH), ("ab1", NH)):
    COL[_name] = (_at, _at + _n)
    _at += _n
NSMALL = _at
NW = 3 * D + D + F
NROW = 3 * D + D + D
NPROB = 6


def schedule():
    def before(b):
        return ([("norm1", b, c) for c in range(2)] + [("proj", b, n) for n in range(NT)]
                + [("tr_qk", b, c) for c in range(3)] + [("proj", b, n) for n in range(NT, NT + 2)])

    groups = [(b, g) for b in range(B) for g in range(NG)]
    turn0 = [("tr_attn", 0, c) for c in range(2)] + [("out", 0, n) for n in range(2)]
    fill = {0: before(1)[:9], 1: before(1)[9:], 3: turn0, 4: [("norm3", 0, c) for c in range(2)]}
    head = [("gn", b, n) for b in range(B) for n in range(2)]
    head = head[:2] + before(0)[:5] + head[2:] + before(0)[5:]
    middle = [("max", 0, h) for h in range(GJ)] + [("maxrow", 0, 0)]
    for i, (b, g) in enumerate(groups):
        if i:
            middle += [("pv", *groups[i - 1]), ("tr_o", *groups[i - 1])]
        more = list(fill.get(i, []))
        nxt = groups[i + 1] if i + 1 < len(groups) else None
        if nxt:
            middle += [("max", nxt[0], GJ * nxt[1])]
        for j in range(GJ):
            if nxt and j + 1 < GJ:
                middle += [("max", nxt[0], GJ * nxt[1] + j + 1)]
            middle += [("exp", b, GJ * g + j)]
            take = -(-len(more) // (GJ - j))
            middle, more = middle + more[:take], more[take:]
            if nxt and j == GJ - 2:
                middle += [("maxrow", *nxt)]
    up0, down0 = [("up", 0, n) for n in range(NF)], [("down", 0, n) for n in range(2)]
    tail = ([("pv", *groups[-1])] + up0[:1] + [("tr_o", *groups[-1])] + up0[1:2]
            + [("tr_attn", 1, c) for c in range(2)] + up0[2:4] + [("out", 1, n) for n in range(2)] + up0[4:]
            + down0 + [("norm3", 1, c) for c in range(2)]
            + [("up", 1, n) for n in range(NF)] + [("down", 1, n) for n in range(2)])
    return head, middle, tail


HEAD, MIDDLE, TAIL = schedule()
STEPS = HEAD + MIDDLE + TAIL
GROUP_LIST = [(b, g) for b in range(B) for g in range(NG)]


def banks():
    bank, turn, before, last = {}, {}, {}, {}
    for part, pool in ((HEAD, 6), (MIDDLE, 2), (TAIL, 6)):
        n = 0
        for step in part:
            if step[0] in ("max", "exp"):
                continue
            k = n % pool
            n += 1
            bank[step] = k
            before[step] = last.get(k)
            turn[step] = turn[last[k]] + 1 if k in last else 1
            last[k] = step
    return bank, turn, before


BANK, TURN, BEFORE = banks()
HEAD_LAST = {BANK[s]: s for s in HEAD}
CHUNKS = [sorted({64 * g // P, (D + 64 * g) // P}) for g in range(NG)]
LOAD_AFTER = {}
for _b in range(B):
    for _g in range(NG):
        _need = [("tr_qk", _b, CHUNKS[_g][-1])] + ([("exp", 0, GJ * _g + GJ - 1)] if _b else [])
        LOAD_AFTER.setdefault(max(_need, key=STEPS.index), []).append((_b, _g))
NTH = {}
for _s in STEPS:
    NTH[_s] = 1 + sum(1 for t in NTH if t[0] == _s[0])


def build(nc, x, small, wa, wb, w2, rows, keyrows, out):
    ctx = ExitStack()
    with ctx:
        def sb(name, shape, dt=fp32):
            return ctx.enter_context(nc.sbuf_tensor(name, shape, dt))

        def sem(name):
            return ctx.enter_context(nc.semaphore(name))

        x_sb = sb("x_sb", [P, B, NT, D])
        y_sb = sb("y_sb", [P, B, NT, D])
        small_sb = sb("small_sb", [P, NSMALL])
        wa_sb = sb("wa_sb", [KA, NW])
        wb_sb = sb("wb_sb", [KB, NW])
        w2_sb = sb("w2_sb", [P, NF, D])
        rows_sb = sb("rows_sb", [P, NROW])
        keyrows_sb = sb("keyrows_sb", [P, T])
        mean_w = sb("mean_w", [P, P])
        squares = sb("squares", [P, NT, D])
        z_sb = sb("z_sb", [P, NT, D])
        nt_a = sb("nt_a", [KA, T])
        nt_b = sb("nt_b", [KB, T])
        n3_a = sb("n3_a", [KA, T])
        n3_b = sb("n3_b", [KB, T])
        qk_sb = sb("qk_sb", [P, NT, 2 * NH, HD])
        rot = sb("rot", [P, 2 * NH, 2, 4])
        rot2 = sb("rot2", [P, 2 * NH, 2, 4])
        v_sb = sb("v_sb", [P, B, NT, NH, VW])
        qk_h = sb("qk_h", [P, 3, T], fp32r)
        qk_l = sb("qk_l", [P, 3, T], fp32r)
        q_st = sb("q_st", [P, NH, T], fp32r)
        k_st = sb("k_st", [P, NH, T], fp32r)
        probs = sb("probs", [P, NPROB, NT, T])
        negmax = sb("negmax", [P, NT, GJ])
        negmax_p = sb("negmax_p", [P, NT, 2, GJ])
        maxrow = sb("maxrow", [2 * GJ, T], fp32r)
        o_sb = sb("o_sb", [P, T])
        rec = sb("rec", [P, NT, GJ])
        attn = sb("attn", [P, NT, D])
        flat = sb("flat", [P, NT, D])
        hid = sb("hid", [P, NF, T])
        res = sb("res", [P, NT, D])
        y_out = sb("y_out", [P, NT, D])
        stat_g = sb("stat_g", [P, 2, GROUPS])
        stat = sb("stat", [P, NT, 6])
        mv = sb("mv", [P, NT, 2])
        newton = sb("newton", [P, 3, GROUPS])
        coef = sb("coef", [P, 4, NH])

        ps_work = [ctx.enter_context(nc.psum_tensor(f"ps_work{i}", [P, T], fp32)) for i in range(2)]
        ps_exp = [ctx.enter_context(nc.psum_tensor(f"ps_exp{i}", [P, 2, T], fp32)) for i in range(2)]
        ps_max = [ctx.enter_context(nc.psum_tensor(f"ps_max{i}", [P, T], fp32)) for i in range(2)]
        ps = [ps_work[0][:, :], ps_work[1][:, :]] + [ps_exp[i][:, k, :] for i in range(2) for k in range(2)]
        scr = nc.dram_tensor("qk_scratch", (B, 2, DQK, T), fp32, kind="Internal").ap()

        x_in = [sem(f"x_in{b}") for b in range(B)]
        small_in = sem("small_in")
        key_in = sem("key_in")
        w_in = sem("w_in")
        w2_in = sem("w2_in")
        rows_in = sem("rows_in")
        filled = [sem(f"filled{i}") for i in range(6)]
        const_ok = sem("const_ok")
        v_ones = sem("v_ones")
        wq_scaled = sem("wq_scaled")
        rows_scaled = sem("rows_scaled")
        centred = sem("centred")
        squared = sem("squared")
        vars_ok = sem("vars_ok")
        gn_ok = sem("gn_ok")
        z_ok = sem("z_ok")
        nt_ok = sem("nt_ok")
        n3_ok = sem("n3_ok")
        proj_ok = sem("proj_ok")
        rope_ok = sem("rope_ok")
        h_ok = sem("h_ok")
        l_ok = sem("l_ok")
        scr_ok = [sem(f"scr_ok{c}") for c in range(3)]
        st_ok = [sem(f"st_ok{g}") for g in range(NG)]
        st_const = sem("st_const")
        st_bias = sem("st_bias")
        coef_ok = sem("coef_ok")
        max_filled = sem("max_filled")
        max_ok = sem("max_ok")
        split_ok = sem("split_ok")
        mrow_ok = sem("mrow_ok")
        st_max = [sem(f"st_max{g}") for g in range(NG)]
        exp_filled = sem("exp_filled")
        exp_ok = sem("exp_ok")
        o_ok = sem("o_ok")
        attn_ok = sem("attn_ok")
        flat_ok = sem("flat_ok")
        ybo_ok = sem("ybo_ok")
        xb2_ok = sem("xb2_ok")
        res_ok = sem("res_ok")
        hid_ok = sem("hid_ok")
        out_ok = sem("out_ok")
        stored = sem("stored")
        dve_chain = sem("dve_chain")
        block = ctx.enter_context(nc.Block())

        read = {"norm1": nt_ok, "tr_attn": nt_ok, "norm3": n3_ok, "proj": proj_ok, "tr_qk": l_ok,
                "maxrow": mrow_ok, "pv": o_ok, "tr_o": attn_ok, "out": flat_ok, "up": hid_ok, "down": out_ok}

        def wait_read(eng, step):
            kind, b, n = step
            if kind == "gn":
                eng.wait_ge((centred, vars_ok)[n], b + 1)
            elif kind in ("norm1", "tr_attn"):
                eng.wait_ge(nt_ok, nt_turn(step))
            else:
                eng.wait_ge(read[kind], NTH[step])

        def nt_turn(step):
            return NTH[step] + (2 * B if step[0] == "tr_attn" else 0)

        def wait_filled(eng, step):
            eng.wait_ge(filled[BANK[step]], TURN[step])

        def col(name, rows_=slice(None)):
            return small_sb[rows_, COL[name][0]:COL[name][1]]

        def view(ap, *dims):
            return bass.AP(tensor=ap.tensor, offset=ap.offset, ap=[list(ap.ap[0]), *[list(d) for d in dims]])

        def work(step):
            return ps[BANK[step]]

        @block.sync
        def _(sp):
            tokens = "b (v c) s d -> b (c s) v d"
            xv, ov = x.rearrange(tokens, v=NT), out.rearrange(tokens, v=NT)
            sp.dma_start(x_sb[:, 0], xv[0]).then_inc(x_in[0], 16)
            sp.dma_start(x_sb[:, 1], xv[1]).then_inc(x_in[1], 16)
            sp.dma_start(rows_sb[:], rows.partition_broadcast(P)).then_inc(rows_in, 16)
            sp.dma_start(w2_sb[:], w2).then_inc(w2_in, 16)
            sp.wait_ge(key_in, 16)
            sp.dma_start(k_st[ROW_BIAS:ROWS, :, :].bitcast(fp32),
                         view(keyrows_sb[ROW_BIAS:ROWS, :], [0, NH], [1, T])).then_inc(st_const, 16)

            def load_group(b, g):
                for c in CHUNKS[g]:
                    sp.wait_ge(scr_ok[c], 32 * (b + 1))
                if b:
                    sp.wait_ge(exp_ok, 2 * GJ * (g + 1))
                for part_q, part_k, row in ((0, 0, 0), (0, 1, 16), (1, 0, 32), (1, 1, 48)):
                    for st, part, at in ((q_st, part_q, 64 * g), (k_st, part_k, D + 64 * g)):
                        src = scr[b, part, at:at + 64, :].rearrange("(h r) t -> r h t", h=GJ)
                        sp.dma_start(st[row:row + 16, GJ * g:GJ * (g + 1), :].bitcast(fp32), src)\
                          .then_inc(st_ok[g], 16)

            for step in STEPS:
                kind, b, n = step
                if kind == "tr_qk":
                    for part, (src, ok) in enumerate(((qk_h, h_ok), (qk_l, l_ok))):
                        sp.wait_ge(ok, 3 * b + n + 1)
                        sp.dma_start(scr[b, part, P * n:P * (n + 1), :], src[:, n, :].bitcast(fp32))\
                          .then_inc(scr_ok[n], 16)
                if kind == "maxrow":
                    sp.wait_ge(mrow_ok, NG * b + n + 1)
                    for part in range(2):
                        dst = q_st[ROW_MAX + part:ROW_MAX + part + 1, GJ * n:GJ * (n + 1), :].bitcast(fp32)
                        sp.dma_start(dst, maxrow[GJ * part:GJ * (part + 1), :].bitcast(fp32)).then_inc(st_max[n], 16)
                for lb, lg in LOAD_AFTER.get(step, []):
                    load_group(lb, lg)
                if kind == "down":
                    sp.wait_ge(out_ok, 2 * b + n + 1)
                    sp.dma_start(ov[b][:, 2 * n:2 * n + 2], y_out[:, 2 * n:2 * n + 2, :]).then_inc(stored, 16)
            sp.wait_ge(stored, 16 * 2 * B)

        @block.gpsimd
        def _(pool):
            pool.memset(mean_w[:], 1.0 / (T * GW)).then_inc(const_ok, 1)
            pool.memset(v_sb[:], 1.0).then_inc(v_ones, 1)
            pool.wait_ge(rows_in, 16)
            for step in STEPS:
                kind, b, n = step
                if kind == "norm1" and n == 1:
                    pool.wait_ge(centred, b + 1)
                    b2r = view(rows_sb[:, NROW - D:NROW], [0, NT], [1, D])
                    pool.tensor_tensor(x_sb[:, b], x_sb[:, b], b2r, ALU.add).then_inc(xb2_ok, 1)
                    pool.wait_ge(z_ok, b + 1)
                    bor = view(rows_sb[:, 3 * D:4 * D], [0, NT], [1, D])
                    pool.tensor_tensor(y_sb[:, b], y_sb[:, b], bor, ALU.add).then_inc(ybo_ok, 1)
                if kind == "out" and n == 1:
                    pool.wait_ge(flat_ok, 2 * b + 2)
                    pool.wait_ge(xb2_ok, b + 1)
                    if b:
                        pool.wait_ge(out_ok, 2 * b)
                    pool.tensor_tensor(res[:], flat[:], x_sb[:, b], ALU.add).then_inc(res_ok, 1)

        @block.scalar
        def _(act):
            act.dma_start(small_sb[:], small).then_inc(small_in, 16)
            act.dma_start(keyrows_sb[ROW_BIAS:ROWS, :], keyrows).then_inc(key_in, 16)
            act.dma_start(wa_sb[:], wa).then_inc(w_in, 16)
            act.dma_start(wb_sb[:], wb).then_inc(w_in, 16)
            exps = 0
            for step in STEPS:
                kind, b, n = step
                if kind == "gn" and n == 0:
                    act.wait_ge(centred, b + 1)
                    if b:
                        wait_filled(act, ("gn", 0, 1))
                    act.activation(squares[:], y_sb[:, b], ACT.Square).then_inc(squared, 1)
                if step == ("gn", 0, 1):
                    act.wait_ge(w_in, 32)
                    for w in (wa_sb, wb_sb):
                        act.mul(w[:, 0:D], w[:, 0:D], HD ** -0.5).then_inc(wq_scaled, 1)
                    act.wait_ge(rows_in, 16)
                    act.mul(rows_sb[:, 0:D], rows_sb[:, 0:D], HD ** -0.5).then_inc(rows_scaled, 1)
                    act.wait_ge(coef_ok, 1)
                    act.wait_ge(key_in, 16)
                    for h in range(NH):
                        act.activation(q_st[ROW_BIAS:ROW_MAX, h, :], keyrows_sb[ROW_BIAS:ROW_MAX, :], ACT.Copy,
                                       scale=coef[ROW_BIAS:ROW_MAX, 3, h:h + 1]).then_inc(st_bias, 1)
                if kind in ("norm1", "norm3"):
                    act.wait_ge(small_in, 16)
                    wait_filled(act, step)
                    k = kind[-1]
                    m = (KA, KB)[n]
                    dst = ((nt_a, nt_b) if k == "1" else (n3_a, n3_b))[n]
                    if b:
                        wait_filled(act, ("proj", 0, NT + 1) if k == "1" else ("up", 0, NF - 1))
                    act.activation(dst[:], work(step)[0:m, :], ACT.Identity, scale=col("g" + k, slice(0, m))[:, n:n + 1],
                                   bias=col("c" + k, slice(0, m))[:, n:n + 1]).then_inc(nt_ok if k == "1" else n3_ok, 1)
                if kind == "tr_qk":
                    wait_filled(act, step)
                    if b:
                        act.wait_ge(scr_ok[n], 32)
                    act.activation(qk_h[:, n, :], work(step), ACT.Copy).then_inc(h_ok, 1)
                if kind == "maxrow":
                    wait_filled(act, step)
                    if NTH[step] > 1:
                        pb, pg = GROUP_LIST[NTH[step] - 2]
                        act.wait_ge(st_max[pg], 32 * (pb + 1))
                    act.activation(maxrow[:], work(step)[0:2 * GJ, :], ACT.Copy).then_inc(mrow_ok, 1)
                if kind == "exp":
                    head = NH * b + n
                    if head >= NPROB:
                        wait_filled(act, ("pv", *GROUP_LIST[(head - NPROB) // GJ]))
                    for half in range(2):
                        exps += 1
                        act.wait_ge(exp_filled, exps)
                        act.activation(probs[:, head % NPROB, 2 * half:2 * half + 2, :], ps_exp[(exps - 1) % 2][:],
                                       ACT.Exp).then_inc(exp_ok, 1)
                if kind == "pv":
                    wait_filled(act, step)
                    if NTH[step] > 1:
                        wait_filled(act, ("tr_o", *GROUP_LIST[NTH[step] - 2]))
                    act.activation(o_sb[:], work(step), ACT.Copy).then_inc(o_ok, 1)
                if kind == "tr_attn":
                    wait_filled(act, step)
                    wait_filled(act, ("proj", 1, NT + 1) if b == 0 else ("out", 0, 1))
                    m, dst = ((KA, nt_a), (KB, nt_b))[n]
                    act.activation(dst[:], work(step)[0:m, :], ACT.Copy).then_inc(nt_ok, 1)
                if kind == "up":
                    wait_filled(act, step)
                    if b:
                        wait_filled(act, ("down", 0, 1))
                    act.activation(hid[:, n, :], work(step), ACT.Gelu, bias=col("b1")[:, n:n + 1]).then_inc(hid_ok, 1)

        @block.tensor
        def _(pe):
            ident = col("ident")

            def turn(step, src, m):
                for t in range(NT):
                    mm = pe.transpose(work(step)[0:m, P * t:P * (t + 1)], src(t), ident)
                return mm

            def contract(dst, a, b_, tokens, lo, hi):
                pe.matmul(dst, a[:, tokens], wa_sb[:, lo:hi], start=True, stop=False)
                return pe.matmul(dst, b_[:, tokens], wb_sb[:, lo:hi], start=False, stop=True)

            def tile(t):
                return slice(P * t, P * (t + 1))

            pe.wait_ge(const_ok, 1)
            maxs = exps = 0
            for step in STEPS:
                kind, b, n = step
                if kind not in ("max", "exp"):
                    if BEFORE[step]:
                        wait_read(pe, BEFORE[step])
                    if step in TAIL and BANK[step] >= 2:
                        pe.wait_ge(exp_ok, 2 * NH * B)
                    w = work(step)
                if kind == "gn":
                    if n == 0:
                        pe.wait_ge(x_in[b], 16)
                    else:
                        pe.wait_ge(squared, b + 1)
                    for t in range(NT):
                        mm = pe.matmul(w[:, 0:D], mean_w[:], x_sb[:, b, t, :] if n == 0 else squares[:, t, :],
                                       start=(t == 0), stop=(t == NT - 1))
                if kind in ("norm1", "norm3"):
                    if n == 0:
                        pe.wait_ge(small_in, 16)
                        pe.wait_ge(z_ok, b + 1 if kind == "norm1" else B + b + 1)
                    lo, hi = ((0, KA), (KA, D))[n]
                    mm = turn(step, lambda t: z_sb[:, t, lo:hi], hi - lo)
                if kind == "proj":
                    pe.wait_ge(nt_ok, 2 * b + 2)
                    pe.wait_ge(wq_scaled, 2)
                    if n < NT:
                        mm = contract(w[:, 0:DQK], nt_a, nt_b, tile(n), 0, DQK)
                    else:
                        for k in range(2):
                            mm = contract(w[:, D * k:D * (k + 1)], nt_a, nt_b, tile(2 * (n - NT) + k), DQK, 3 * D)
                if kind == "tr_qk":
                    pe.wait_ge(rope_ok, NT * (b + 1))
                    mm = turn(step, lambda t: qk_sb[:, t, 8 * n:8 * (n + 1), :].rearrange("p h d -> p (h d)"), P)
                if kind == "maxrow":
                    pe.wait_ge(split_ok, NTH[step])
                    mm = turn(step, lambda t: negmax_p[:, t].rearrange("p a j -> p (a j)"), 2 * GJ)
                if kind == "max":
                    g = n // GJ
                    pe.wait_ge(st_ok[g], 128 * (b + 1))
                    pe.wait_ge(st_const, 16)
                    pe.wait_ge(st_bias, n + 1)
                    for t in range(NT):
                        if maxs >= 2:
                            pe.wait_ge(max_ok, maxs - 1)
                        pe.matmul(ps_max[maxs % 2][:], q_st[0:ROW_MAX, n, tile(t)], k_st[0:ROW_MAX, n, :],
                                  start=True, stop=True).then_inc(max_filled, 1)
                        maxs += 1
                if kind == "exp":
                    pe.wait_ge(st_max[n // GJ], 32 * (b + 1))
                    for half in range(2):
                        if exps >= 2:
                            pe.wait_ge(exp_ok, exps - 1)
                        else:
                            for k in range(2):
                                if 2 + 2 * exps + k in HEAD_LAST:
                                    wait_read(pe, HEAD_LAST[2 + 2 * exps + k])
                        for k in range(2):
                            mm = pe.matmul(ps_exp[exps % 2][:, k, :], k_st[0:ROWS, n, tile(2 * half + k)],
                                           q_st[0:ROWS, n, :], start=True, stop=True)
                        mm.then_inc(exp_filled, 1)
                        exps += 1
                if kind == "pv":
                    pe.wait_ge(proj_ok, (NT + 2) * (b + 1))
                    pe.wait_ge(exp_ok, 2 * (NH * b + GJ * (n + 1)))
                    for t in range(NT):
                        for j in range(GJ):
                            h = GJ * n + j
                            mm = pe.matmul(w[VW * j:VW * (j + 1), :], v_sb[:, b, t, h, :],
                                           probs[:, (NH * b + h) % NPROB, t, :], start=(t == 0), stop=(t == NT - 1),
                                           tile_position=(0, VW * j))
                if kind == "tr_o":
                    pe.wait_ge(o_ok, NTH[step])
                    mm = turn(step, lambda t: o_sb[:, tile(t)], P)
                if kind == "tr_attn":
                    pe.wait_ge(attn_ok, NG * (b + 1))
                    lo, hi = ((0, KA), (KA, D))[n]
                    mm = turn(step, lambda t: attn[:, t, lo:hi], hi - lo)
                if kind == "out":
                    pe.wait_ge(nt_ok, 2 * B + 2 * (b + 1))
                    for k in range(2):
                        mm = contract(w[:, D * k:D * (k + 1)], nt_a, nt_b, tile(2 * n + k), 3 * D, 4 * D)
                if kind == "up":
                    pe.wait_ge(n3_ok, 2 * (b + 1))
                    lo, hi = 4 * D + P * n, 4 * D + P * (n + 1)
                    pe.matmul(w, wa_sb[:, lo:hi], n3_a[:], start=True, stop=False)
                    mm = pe.matmul(w, wb_sb[:, lo:hi], n3_b[:], start=False, stop=True)
                if kind == "down":
                    pe.wait_ge(w2_in, 16)
                    pe.wait_ge(hid_ok, NF * (b + 1))
                    for k in range(2):
                        for f in range(NF):
                            mm = pe.matmul(w[:, D * k:D * (k + 1)], hid[:, f, tile(2 * n + k)], w2_sb[:, f, :],
                                           start=(f == 0), stop=(f == NF - 1))
                if kind not in ("max", "exp"):
                    mm.then_inc(filled[BANK[step]], 1)

        @block.vector
        def _(dve):
            links = [0]

            def link(ins):
                links[0] += 1
                ins.then_inc(dve_chain, 1)
                dve.wait_ge(dve_chain, links[0])

            def rsqrt(dst, var, n):
                v, t = newton[:, 0, 0:n], newton[:, 1, 0:n]
                link(dve.tensor_scalar(v, var, EPS, None, ALU.add))
                link(dve.tensor_scalar(t.bitcast(int32), v.bitcast(int32), 1, None, ALU.logical_shift_right))
                link(dve.tensor_scalar(dst.bitcast(int32), t.bitcast(int32), -1.0, float(0x5f3759df), ALU.mult, ALU.add))
                for _ in range(4):
                    link(dve.tensor_tensor(t, dst, dst, ALU.mult))
                    link(dve.scalar_tensor_tensor(out=t, in0=t, scalar=-0.5, in1=v, op0=ALU.mult, op1=ALU.mult))
                    link(dve.scalar_tensor_tensor(out=dst, in0=t, scalar=1.5, in1=dst, op0=ALU.add, op1=ALU.mult))

            def layer_norm(src):
                for t in range(NT):
                    ins = dve.bn_stats(stat[:, t, :], src[:, t, :])
                    ins.then_inc(dve_chain, 1)
                    links[0] += 1
                dve.wait_ge(dve_chain, links[0])
                for t in range(NT):
                    ins = dve.bn_aggr(mv[:, t, :], stat[:, t, :])
                    ins.then_inc(dve_chain, 1)
                    links[0] += 1
                dve.wait_ge(dve_chain, links[0])
                rstd = newton[:, 2, 0:NT]
                rsqrt(rstd, mv[:, :, 1], NT)
                for t in range(NT):
                    ins = dve.tensor_scalar(z_sb[:, t, :], src[:, t, :], mv[:, t, 0:1], rstd[:, t:t + 1],
                                            ALU.subtract, ALU.mult)
                    if t < NT - 1:
                        ins.then_inc(dve_chain, 1)
                        links[0] += 1
                dve.wait_ge(dve_chain, links[0])
                ins.then_inc(z_ok, 1)

            dve.wait_ge(small_in, 16)
            r = slice(ROW_BIAS, ROW_MAX)
            link(dve.tensor_scalar(coef[r, 0, :], col("ab0", r), col("ca", r), None, ALU.mult))
            link(dve.scalar_tensor_tensor(out=coef[r, 1, :], in0=col("ab1", r), scalar=col("cb", r),
                                          in1=coef[r, 0, :], op0=ALU.mult, op1=ALU.add))
            link(dve.tensor_copy(coef[r, 2, :].bitcast(fp32r), coef[r, 1, :]))
            link(dve.tensor_scalar(coef[r, 0, :], coef[r, 2, :], col("low", r), None, ALU.mult))
            dve.tensor_tensor(coef[r, 3, :], coef[r, 1, :], coef[r, 0, :], ALU.subtract).then_inc(coef_ok, 1)

            maxs = 0
            for step in STEPS:
                kind, b, n = step
                if kind == "gn" and n == 0:
                    wait_filled(dve, step)
                    link(dve.tensor_reduce(stat_g[:, 0, :], view(work(step), [GW, GROUPS], [1, GW]), AX.X, ALU.add))
                    dve.tensor_tensor(y_sb[:, b], view(x_sb[:, b], [D, NT], [GW, GROUPS], [1, GW]),
                                      view(stat_g[:, 0, :], [0, NT], [1, GROUPS], [0, GW]), ALU.subtract)\
                       .then_inc(centred, 1)
                if kind == "gn" and n == 1:
                    wait_filled(dve, step)
                    dve.tensor_reduce(stat_g[:, 0, :], view(work(step), [GW, GROUPS], [1, GW]), AX.X, ALU.add)\
                       .then_inc(vars_ok, 1)
                    dve.wait_ge(vars_ok, b + 1)
                    rsqrt(stat_g[:, 1, :], stat_g[:, 0, :], GROUPS)
                    dve.wait_ge(squared, b + 1)
                    yv = view(y_sb[:, b], [D, NT], [GW, GROUPS], [1, GW])
                    dve.tensor_tensor(yv, yv, view(stat_g[:, 1, :], [0, NT], [1, GROUPS], [0, GW]), ALU.mult)\
                       .then_inc(gn_ok, 1)
                    dve.wait_ge(gn_ok, b + 1)
                    if b:
                        wait_filled(dve, ("norm1", 0, 1))
                    layer_norm(y_sb[:, b])
                if kind == "proj":
                    wait_filled(dve, step)
                    dve.wait_ge(rows_scaled, 1)
                    if n < NT:
                        if b:
                            wait_filled(dve, ("tr_qk", b - 1, 2))
                        dve.tensor_tensor(qk_sb[:, n].rearrange("p h d -> p (h d)"), work(step)[:, 0:DQK],
                                          rows_sb[:, 0:DQK], ALU.add).then_inc(proj_ok, 1)
                        dve.wait_ge(proj_ok, NTH[step])
                        low, high = qk_sb[:, n, :, 0:4], qk_sb[:, n, :, 8:12]
                        both = view(qk_sb[:, n], [HD, 2 * NH], [HD // 2, 2], [1, 4])
                        at = slice(4 * n, 4 * n + 4)
                        dve.tensor_tensor(rot[:], both, view(col("cos")[:, at], [0, 2 * NH], [0, 2], [1, 4]), ALU.mult)\
                           .then_inc(dve_chain, 1)
                        dve.tensor_tensor(rot2[:, :, 0, :], high, view(col("nsin")[:, at], [0, 2 * NH], [1, 4]),
                                          ALU.mult).then_inc(dve_chain, 1)
                        dve.tensor_tensor(rot2[:, :, 1, :], low, view(col("sin")[:, at], [0, 2 * NH], [1, 4]),
                                          ALU.mult).then_inc(dve_chain, 1)
                        links[0] += 3
                        dve.wait_ge(dve_chain, links[0])
                        dve.tensor_tensor(both, rot[:], rot2[:], ALU.add).then_inc(rope_ok, 1)
                        dve.wait_ge(rope_ok, NT * b + n + 1)
                    else:
                        dve.wait_ge(v_ones, 1)
                        t = 2 * (n - NT)
                        for k in range(2):
                            ins = dve.tensor_tensor(v_sb[:, b, t + k, :, 0:HD], view(work(step)[:, D * k:D * (k + 1)],
                                                    [HD, NH], [1, HD]), view(rows_sb[:, DQK:3 * D], [HD, NH], [1, HD]),
                                                    ALU.add)
                            if k == 0:
                                link(ins)
                        ins.then_inc(proj_ok, 1)
                if kind == "tr_qk":
                    dve.wait_ge(h_ok, 3 * b + n + 1)
                    if b:
                        dve.wait_ge(scr_ok[n], 32)
                    dve.tensor_tensor(qk_l[:, n, :], work(step), qk_h[:, n, :].bitcast(fp32), ALU.subtract)\
                       .then_inc(l_ok, 1)
                if kind == "max":
                    if n % GJ == 0 and (b or n):
                        dve.wait_ge(split_ok, NG * b + n // GJ)
                    for t in range(NT):
                        maxs += 1
                        dve.wait_ge(max_filled, maxs)
                        dve.tensor_reduce(negmax[:, t, n % GJ:n % GJ + 1], ps_max[(maxs - 1) % 2][:], AX.X, ALU.max,
                                          negate=True).then_inc(max_ok, 1)
                if kind == "maxrow":
                    dve.wait_ge(max_ok, maxs)
                    if NTH[step] > 1:
                        wait_filled(dve, ("maxrow", *GROUP_LIST[NTH[step] - 2]))
                    link(dve.tensor_copy(negmax_p[:, :, 0, :].bitcast(fp32r), negmax[:]))
                    dve.tensor_tensor(negmax_p[:, :, 1, :], negmax[:], negmax_p[:, :, 0, :], ALU.subtract)\
                       .then_inc(split_ok, 1)
                if kind == "tr_o":
                    wait_filled(dve, step)
                    if b and n == 0:
                        wait_filled(dve, ("tr_attn", 0, 1))
                    link(dve.reciprocal(rec[:], view(work(step)[:, HD:HD + 1], [P, NT], [VW, GJ])))
                    dve.tensor_tensor(view(attn[:, :, 64 * n:64 * (n + 1)], [D, NT], [HD, GJ], [1, HD]),
                                      view(work(step), [P, NT], [VW, GJ], [1, HD]),
                                      view(rec[:], [GJ, NT], [1, GJ], [0, HD]), ALU.mult).then_inc(attn_ok, 1)
                if kind == "out":
                    wait_filled(dve, step)
                    dve.wait_ge(ybo_ok, b + 1)
                    if b and n == 0:
                        dve.wait_ge(res_ok, b)
                    dve.tensor_tensor(flat[:, 2 * n:2 * n + 2, :], view(work(step), [D, 2], [1, D]),
                                      y_sb[:, b, 2 * n:2 * n + 2, :], ALU.add).then_inc(flat_ok, 1)
                    if n == 1:
                        dve.wait_ge(flat_ok, 2 * b + 2)
                        wait_filled(dve, ("norm1", 1, 1) if b == 0 else ("norm3", 0, 1))
                        layer_norm(flat)
                if kind == "down":
                    wait_filled(dve, step)
                    dve.wait_ge(res_ok, b + 1)
                    if b:
                        dve.wait_ge(stored, 16 * 2 * b)
                    dve.tensor_tensor(y_out[:, 2 * n:2 * n + 2, :], view(work(step), [D, 2], [1, D]),
                                      res[:, 2 * n:2 * n + 2, :], ALU.add).then_inc(out_ok, 1)


def kernel(**inputs):
    import numpy as np
    import concourse.bacc as bacc
    from concourse.bass_utils import run_bass_kernel_spmd as run

    p = {k.removeprefix("L0_conv_"): np.asarray(v) for k, v in inputs.items()}
    f = np.float32

    def chunks(v):
        a = np.zeros((P, 2), f)
        a[:, 0] = v[:KA]
        a[:KB, 1] = v[KA:]
        return a

    fraction = f(2.0) * np.arange(4, dtype=f) / f(HD)
    angles = np.arange(T, dtype=f)[:, None] / (f(10000.0) ** fraction).astype(f)[None, :]
    table = {"cos": np.cos(angles), "sin": np.sin(angles), "nsin": -np.sin(angles)}
    table = {k: v.astype(f).reshape(NT, P, 4).transpose(1, 0, 2).reshape(P, NT * 4) for k, v in table.items()}
    row = np.arange(P)
    low = ((row >= ROW_BIAS + C) & (row < ROW_BIAS + 2 * C)) | (row == ROW_BIAS + 2 * C + 1)
    is_b1 = row >= ROW_BIAS + 2 * C
    small = np.concatenate([
        np.eye(P, dtype=f), table["cos"], table["sin"], table["nsin"], chunks(p["ln1_g"]), chunks(p["ln1_b"]),
        chunks(p["ln3_g"]), chunks(p["ln3_b"]), p["b1"].reshape(NF, P).T, low.astype(f)[:, None],
        np.where(is_b1, 0, 1).astype(f)[:, None], np.where(is_b1, 1, -1).astype(f)[:, None],
        np.broadcast_to(p["attn_biases"][:, 0], (P, NH)), np.broadcast_to(p["attn_biases"][:, 1], (P, NH))], axis=1)
    w = np.concatenate([p["wq"], p["wk"], p["wv"], p["wo"], p["w1"]], axis=1)
    onehot = (np.arange(C)[:, None] == np.arange(T)[None, :] // S).astype(f)
    arrays = {
        "x": p["x"], "small": small, "wa": w[:KA], "wb": w[KA:],
        "w2": p["w2"].reshape(NF, P, D).transpose(1, 0, 2),
        "rows": np.concatenate([p[k] for k in ("bq", "bk", "bv", "bo", "b2")]),
        "keyrows": np.concatenate([onehot, onehot, np.ones((ROWS - ROW_BIAS - 2 * C, T), f)]),
    }
    nc = bacc.Bacc("TRN2", target_bir_lowering=False, num_devices=1)
    arrays = {f"in_{k}": np.ascontiguousarray(v) for k, v in arrays.items()}
    args = [nc.dram_tensor(k, v.shape, fp32, kind="ExternalInput").ap() for k, v in arrays.items()]
    out = nc.dram_tensor("out_0", (B, C, S, D), fp32, kind="ExternalOutput").ap()
    build(nc, *args, out)
    return run(nc, [arrays], core_ids=[0]).results[0]["out_0"]
```

```python
import concourse.bass as bass
from concourse import mybir
from contextlib import ExitStack

fp32 = mybir.dt.float32
fp32r = mybir.dt.float32r
int32 = mybir.dt.int32
ALU = mybir.AluOpType
ACT = mybir.ActivationFunctionType
AX = mybir.AxisListType

P = 128
B, C, S, D = 2, 16, 32, 192
T = C * S
NT = T // P
NH, HD = 12, 16
F = 768
NF = F // P
GROUPS, GW = 32, D // 32
GJ = 4
NG = NH // GJ
EPS = 1e-5
KA, KB = P, D - P
DQK = 2 * D

ROW_BIAS, ROW_MAX, ROWS = 64, 98, 100
VW = 32

COL = {}
_at = 0
for _name, _n in (("ident", P), ("cos", NT * 4), ("sin", NT * 4), ("nsin", NT * 4), ("g1", 2), ("c1", 2),
                  ("g3", 2), ("c3", 2), ("b1", NF), ("low", 1), ("ca", 1), ("cb", 1), ("ab0", NH), ("ab1", NH)):
    COL[_name] = (_at, _at + _n)
    _at += _n
NSMALL = _at
NW = 3 * D + D + F
NROW = 3 * D + D + D
NPROB = 6


EXP_LAG = 24


def schedule():
    def norm(b):
        return [("gn", b, 0), ("gn", b, 1), ("scale", b, 0), ("z1", b, 0)]

    head = norm(0) + [("norm1", 0, c) for c in range(2)] + [("proj", 0, n) for n in range(NT)]
    head += [("tr_qk", 0, c) for c in range(3)]
    slots = {}

    def put(k, *steps):
        slots.setdefault(k, []).extend(steps)

    units, per = NH * NT, GJ * NT
    for k in range(B * units):
        b, u = divmod(k, units)
        put(k, ("max", b, u))
        if u % per == per - 1:
            put(k, ("split", b, u // per))
            put(k + 3, ("maxrow", b, u // per))
    for k in range(B * units // 2):
        put(EXP_LAG + 2 * k, ("exp", k // (units // 2), k % (units // 2)))
    for i in range(B * NG):
        b, g = divmod(i, NG)
        done = EXP_LAG + per * (i + 1)
        for t in range(NT):
            put(done + 1 + 2 * t, ("pv", b, NT * g + t))
        if i < B * NG - 1:
            put(done + 2 * NT + 2, ("tr_o", b, g))
    fill = {1: ("proj", 0, NT), 3: ("proj", 0, NT + 1), 4: ("gn", 1, 0), 7: ("gn", 1, 1), 17: ("scale", 1, 0),
            20: ("z1", 1, 0), 22: ("norm1", 1, 0), 23: ("norm1", 1, 1)}
    fill |= {25 + 2 * n: ("proj", 1, n) for n in range(NT)}
    fill |= {34: ("tr_qk", 1, 0), 35: ("tr_qk", 1, 1), 36: ("tr_qk", 1, 2), 38: ("proj", 1, NT), 49: ("proj", 1, NT + 1)}
    turned = EXP_LAG + per * NG + 2 * NT + 2
    fill |= {turned + 3: ("tr_attn", 0, 0), turned + 4: ("tr_attn", 0, 1), turned + 6: ("out", 0, 0),
             turned + 8: ("out", 0, 1), turned + 9: ("stats3", 0, 0), turned + 12: ("z3", 0, 0),
             turned + 14: ("norm3", 0, 0), turned + 15: ("norm3", 0, 1)}
    for k, step in fill.items():
        put(k, step)
    middle = [step for k in sorted(slots) for step in slots[k]]
    up0, up1 = ([("up", b, n) for n in range(NF)] for b in range(B))
    tail = (up0[:2] + [("tr_o", B - 1, NG - 1)] + up0[2:3] + [("tr_attn", 1, c) for c in range(2)] + up0[3:5]
            + [("out", 1, n) for n in range(2)] + [("stats3", 1, 0), ("z3", 1, 0)] + up0[5:]
            + [("down", 0, n) for n in range(2)] + [("norm3", 1, c) for c in range(2)] + up1
            + [("down", 1, n) for n in range(2)])
    return head, middle, tail


HEAD, MIDDLE, TAIL = schedule()
STEPS = HEAD + MIDDLE + TAIL
GROUP_LIST = [(b, g) for b in range(B) for g in range(NG)]
FILLING = ("gn", "norm1", "norm3", "proj", "tr_qk", "maxrow", "pv", "tr_o", "tr_attn", "out", "up", "down")


def banks():
    bank, turn, before, last = {}, {}, {}, {}
    for part in (HEAD, MIDDLE, TAIL):
        n = 0
        for step in part:
            kind, b, i = step
            if kind not in FILLING:
                continue
            if kind == "pv" and i % NT:
                for table in (bank, turn):
                    table[step] = table[(kind, b, i - 1)]
                continue
            if part is MIDDLE:
                k = 0 if kind in ("pv", "tr_o") else 1
            else:
                k = n % 8
                n += 1
            bank[step] = k
            before[step] = last.get(k)
            turn[step] = turn[last[k]] + 1 if k in last else 1
            last[k] = step
    return bank, turn, before


BANK, TURN, BEFORE = banks()
HEAD_LAST = {BANK[s]: s for s in HEAD if s in BANK}
CHUNKS = [sorted({HD * h // P, (D + HD * h) // P}) for h in range(NH)]
LOAD_AFTER = {}
for _b in range(B):
    for _h in range(NH):
        _need = [("tr_qk", _b, CHUNKS[_h][-1])] + ([("exp", 0, 2 * _h + 1)] if _b else [])
        LOAD_AFTER.setdefault(max(_need, key=STEPS.index), []).append((_b, _h))
NTH = {}
for _s in STEPS:
    NTH[_s] = 1 + sum(1 for t in NTH if t[0] == _s[0])
for _s in STEPS:
    if _s[0] == "pv":
        NTH[_s] = NG * _s[1] + _s[2] // NT + 1


def build(nc, x, small, wa, wb, w2, rows, keyrows, out):
    ctx = ExitStack()
    with ctx:
        def sb(name, shape, dt=fp32):
            return ctx.enter_context(nc.sbuf_tensor(name, shape, dt))

        def sem(name):
            return ctx.enter_context(nc.semaphore(name))

        x_sb = sb("x_sb", [P, B, NT, D])
        y_sb = sb("y_sb", [P, B, NT, D])
        small_sb = sb("small_sb", [P, NSMALL])
        wa_sb = sb("wa_sb", [KA, NW])
        wb_sb = sb("wb_sb", [KB, NW])
        w2_sb = sb("w2_sb", [P, NF, D])
        rows_sb = sb("rows_sb", [P, NROW])
        keyrows_sb = sb("keyrows_sb", [P, T])
        mean_w = sb("mean_w", [P, P])
        squares = sb("squares", [P, NT, D])
        z_sb = sb("z_sb", [P, NT, D])
        nt_a = sb("nt_a", [KA, T])
        nt_b = sb("nt_b", [KB, T])
        n3_a = sb("n3_a", [KA, T])
        n3_b = sb("n3_b", [KB, T])
        qk_sb = sb("qk_sb", [P, NT, 2 * NH, HD])
        rot = sb("rot", [P, 2 * NH, 2, 4])
        rot2 = sb("rot2", [P, 2 * NH, 2, 4])
        v_sb = sb("v_sb", [P, B, NT, NH, VW])
        qk_h = sb("qk_h", [P, 3, T], fp32r)
        qk_l = sb("qk_l", [P, 3, T], fp32r)
        q_st = sb("q_st", [P, NH, T], fp32r)
        k_st = sb("k_st", [P, NH, T], fp32r)
        probs = sb("probs", [P, NPROB, NT, T])
        negmax = sb("negmax", [P, NT, GJ])
        negmax_p = sb("negmax_p", [P, NT, 2, GJ])
        maxrow = sb("maxrow", [2 * GJ, T], fp32r)
        o_sb = sb("o_sb", [P, T])
        rec = sb("rec", [P, NT, GJ])
        attn = sb("attn", [P, NT, D])
        flat = sb("flat", [P, NT, D])
        hid = sb("hid", [P, NF, T])
        res = sb("res", [P, NT, D])
        y_out = sb("y_out", [P, NT, D])
        stat_g = sb("stat_g", [P, 2, GROUPS])
        stat = sb("stat", [P, NT, 6])
        mv = sb("mv", [P, NT, 2])
        newton = sb("newton", [P, 2, GROUPS])
        rstd = sb("rstd", [P, NT])
        pool_v = sb("pool_v", [P, GROUPS])
        half = sb("half", [P, GROUPS])
        coef = sb("coef", [P, 4, NH])

        ps_work = [ctx.enter_context(nc.psum_tensor(f"ps_work{i}", [P, T], fp32)) for i in range(2)]
        ps_exp = [ctx.enter_context(nc.psum_tensor(f"ps_exp{i}", [P, 2, T], fp32)) for i in range(2)]
        ps_max = [ctx.enter_context(nc.psum_tensor(f"ps_max{i}", [P, T], fp32)) for i in range(2)]
        ps = [ps_work[0][:, :], ps_work[1][:, :]] + [ps_exp[i][:, k, :] for i in range(2) for k in range(2)]
        ps += [ps_max[0][:, :], ps_max[1][:, :]]
        scr = nc.dram_tensor("qk_scratch", (B, 2 * NH, 3 * HD, T), fp32, kind="Internal").ap()

        x_in = [sem(f"x_in{b}") for b in range(B)]
        small_in = sem("small_in")
        key_in = sem("key_in")
        w_in = sem("w_in")
        w2_in = sem("w2_in")
        rows_in = sem("rows_in")
        filled = [sem(f"filled{i}") for i in range(8)]
        const_ok = sem("const_ok")
        v_ones = sem("v_ones")
        wq_scaled = sem("wq_scaled")
        rows_scaled = sem("rows_scaled")
        centred = sem("centred")
        stats_ok = sem("stats_ok")
        rstd_ok = sem("rstd_ok")
        eps_ok = sem("eps_ok")
        squared = sem("squared")
        vars_ok = sem("vars_ok")
        gn_ok = sem("gn_ok")
        z_ok = sem("z_ok")
        nt_ok = sem("nt_ok")
        n3_ok = sem("n3_ok")
        proj_ok = sem("proj_ok")
        rope_ok = sem("rope_ok")
        h_ok = sem("h_ok")
        l_ok = sem("l_ok")
        scr_ok = [sem(f"scr_ok{c}") for c in range(3)]
        st_ok = [sem(f"st_ok{h}") for h in range(NH)]
        st_const = sem("st_const")
        st_bias = sem("st_bias")
        coef_ok = sem("coef_ok")
        max_filled = sem("max_filled")
        max_ok = sem("max_ok")
        split_ok = sem("split_ok")
        mrow_ok = sem("mrow_ok")
        st_max = [sem(f"st_max{g}") for g in range(NG)]
        exp_filled = sem("exp_filled")
        exp_ok = sem("exp_ok")
        o_ok = sem("o_ok")
        attn_ok = sem("attn_ok")
        flat_ok = sem("flat_ok")
        ybo_ok = sem("ybo_ok")
        xb2_ok = sem("xb2_ok")
        res_ok = sem("res_ok")
        hid_ok = sem("hid_ok")
        out_ok = sem("out_ok")
        stored = sem("stored")
        pool_chain = sem("pool_chain")
        dve_chain = sem("dve_chain")
        block = ctx.enter_context(nc.Block())

        read = {"norm1": nt_ok, "tr_attn": nt_ok, "norm3": n3_ok, "proj": proj_ok, "tr_qk": l_ok,
                "maxrow": mrow_ok, "pv": o_ok, "tr_o": attn_ok, "out": flat_ok, "up": hid_ok, "down": out_ok}

        def wait_read(eng, step):
            kind, b, n = step
            if kind == "gn":
                eng.wait_ge((centred, vars_ok)[n], b + 1)
            elif kind in ("norm1", "tr_attn"):
                eng.wait_ge(nt_ok, nt_turn(step))
            else:
                eng.wait_ge(read[kind], NTH[step])

        def nt_turn(step):
            return NTH[step] + (2 * B if step[0] == "tr_attn" else 0)

        def wait_filled(eng, step):
            eng.wait_ge(filled[BANK[step]], TURN[step])

        def col(name, rows_=slice(None)):
            return small_sb[rows_, COL[name][0]:COL[name][1]]

        def view(ap, *dims):
            return bass.AP(tensor=ap.tensor, offset=ap.offset, ap=[list(ap.ap[0]), *[list(d) for d in dims]])

        def work(step):
            return ps[BANK[step]]

        WRITES = (32, 48, 48)

        @block.sync
        def _(sp):
            tokens = "b (v c) s d -> b (c s) v d"
            xv, ov = x.rearrange(tokens, v=NT), out.rearrange(tokens, v=NT)
            sp.dma_start(x_sb[:, 0], xv[0]).then_inc(x_in[0], 16)
            sp.dma_start(x_sb[:, 1], xv[1]).then_inc(x_in[1], 16)
            sp.dma_start(rows_sb[:], rows.partition_broadcast(P)).then_inc(rows_in, 16)
            sp.dma_start(w2_sb[:], w2).then_inc(w2_in, 16)
            sp.wait_ge(key_in, 16)
            sp.dma_start(k_st[ROW_BIAS:ROWS, :, :].bitcast(fp32),
                         view(keyrows_sb[ROW_BIAS:ROWS, :], [0, NH], [1, T])).then_inc(st_const, 16)

            def load_head(b, h):
                for c in CHUNKS[h]:
                    sp.wait_ge(scr_ok[c], WRITES[c] * (b + 1))
                if b:
                    sp.wait_ge(exp_ok, 2 * (h + 1))
                for st, at, step_, start in ((q_st, h, 0, 1), (k_st, NH + h, 1, 0)):
                    src = scr[b, at, HD * start:HD * (start + 1), :]
                    src = bass.AP(tensor=src.tensor, offset=src.offset, ap=[[step_ * HD * T, 2], [T, 2 * HD], [1, T]])
                    sp.dma_start(st[0:ROW_BIAS, h, :].bitcast(fp32), src).then_inc(st_ok[h], 16)

            for step in STEPS:
                kind, b, n = step
                if kind == "tr_qk":
                    heads = P // HD
                    keys = max(NH, heads * n) - heads * n
                    for src, ok, row, first in ((qk_h, h_ok, 1, 0), (qk_l, l_ok, 2, 0), (qk_l, l_ok, 0, keys)):
                        if first < heads:
                            sp.wait_ge(ok, 3 * b + n + 1)
                            dst = scr[b, heads * n + first:heads * (n + 1), HD * row:HD * (row + 1), :]
                            sp.dma_start(dst, src[HD * first:P, n, :].bitcast(fp32)).then_inc(scr_ok[n], 16)
                for lb, lh in LOAD_AFTER.get(step, []):
                    load_head(lb, lh)
                if kind == "maxrow":
                    sp.wait_ge(mrow_ok, NG * b + n + 1)
                    for part in range(2):
                        dst = q_st[ROW_MAX + part:ROW_MAX + part + 1, GJ * n:GJ * (n + 1), :].bitcast(fp32)
                        sp.dma_start(dst, maxrow[GJ * part:GJ * (part + 1), :].bitcast(fp32)).then_inc(st_max[n], 16)
                if kind == "down":
                    sp.wait_ge(out_ok, 2 * b + n + 1)
                    sp.dma_start(ov[b][:, 2 * n:2 * n + 2], y_out[:, 2 * n:2 * n + 2, :]).then_inc(stored, 16)
            sp.wait_ge(stored, 16 * 2 * B)

        @block.gpsimd
        def _(pool):
            pool.memset(mean_w[:], 1.0 / (T * GW)).then_inc(const_ok, 1)
            pool.memset(v_sb[:], 1.0).then_inc(v_ones, 1)
            pool.memset(half[:], -0.5).then_inc(eps_ok, 1)
            pool.wait_ge(rows_in, 16)
            pool.wait_ge(eps_ok, 1)
            rstds = 0

            def rsqrt(dst, var, n):
                v = pool_v[:, 0:n]
                pool.tensor_scalar(v, var, EPS, None, ALU.add).then_inc(pool_chain, 1)
                pool.wait_ge(pool_chain, rstds + 1)
                pool.tensor_tensor(dst, v, half[:, 0:n], ALU.pow).then_inc(rstd_ok, 1)
                pool.wait_ge(rstd_ok, rstds + 1)

            for step in STEPS:
                kind, b, n = step
                if step == ("gn", 1, 1):
                    pool.wait_ge(vars_ok, b + 1)
                    rsqrt(stat_g[:, 1, :], stat_g[:, 0, :], GROUPS)
                    rstds += 1
                if kind in ("scale", "stats3"):
                    pool.wait_ge(stats_ok, b + 1 + (B if kind == "stats3" else 0))
                    rsqrt(rstd[:], mv[:, :, 1], NT)
                    rstds += 1
                if kind == "norm1" and n == 1:
                    pool.wait_ge(centred, b + 1)
                    b2r = view(rows_sb[:, NROW - D:NROW], [0, NT], [1, D])
                    pool.tensor_tensor(x_sb[:, b], x_sb[:, b], b2r, ALU.add).then_inc(xb2_ok, 1)
                    pool.wait_ge(z_ok, NT * (b + 1))
                    bor = view(rows_sb[:, 3 * D:4 * D], [0, NT], [1, D])
                    pool.tensor_tensor(y_sb[:, b], y_sb[:, b], bor, ALU.add).then_inc(ybo_ok, 1)
                if kind == "z3":
                    pool.wait_ge(flat_ok, 2 * b + 2)
                    pool.wait_ge(xb2_ok, b + 1)
                    if b:
                        pool.wait_ge(out_ok, 2 * b)
                    pool.tensor_tensor(res[:], flat[:], x_sb[:, b], ALU.add).then_inc(res_ok, 1)

        @block.scalar
        def _(act):
            act.dma_start(small_sb[:], small).then_inc(small_in, 16)
            act.dma_start(keyrows_sb[ROW_BIAS:ROWS, :], keyrows).then_inc(key_in, 16)
            act.dma_start(wa_sb[:], wa).then_inc(w_in, 16)
            act.dma_start(wb_sb[:], wb).then_inc(w_in, 16)
            exps = 0
            for step in STEPS:
                kind, b, n = step
                if kind == "gn" and n == 0:
                    act.wait_ge(centred, b + 1)
                    if b:
                        wait_filled(act, ("gn", 0, 1))
                    act.activation(squares[:], y_sb[:, b], ACT.Square).then_inc(squared, 1)
                if step == ("gn", 0, 1):
                    act.wait_ge(w_in, 32)
                    for w in (wa_sb, wb_sb):
                        act.mul(w[:, 0:D], w[:, 0:D], HD ** -0.5).then_inc(wq_scaled, 1)
                    act.wait_ge(rows_in, 16)
                    act.mul(rows_sb[:, 0:D], rows_sb[:, 0:D], HD ** -0.5).then_inc(rows_scaled, 1)
                    act.wait_ge(coef_ok, 1)
                    act.wait_ge(key_in, 16)
                    for h in range(NH):
                        act.activation(q_st[ROW_BIAS:ROW_MAX, h, :], keyrows_sb[ROW_BIAS:ROW_MAX, :], ACT.Copy,
                                       scale=coef[ROW_BIAS:ROW_MAX, 3, h:h + 1]).then_inc(st_bias, 1)
                if kind in ("norm1", "norm3"):
                    act.wait_ge(small_in, 16)
                    wait_filled(act, step)
                    k = kind[-1]
                    m = (KA, KB)[n]
                    dst = ((nt_a, nt_b) if k == "1" else (n3_a, n3_b))[n]
                    if b:
                        wait_filled(act, ("proj", 0, NT + 1) if k == "1" else ("up", 0, NF - 1))
                    act.activation(dst[:], work(step)[0:m, :], ACT.Identity, scale=col("g" + k, slice(0, m))[:, n:n + 1],
                                   bias=col("c" + k, slice(0, m))[:, n:n + 1]).then_inc(nt_ok if k == "1" else n3_ok, 1)
                if kind == "tr_qk":
                    wait_filled(act, step)
                    if b:
                        act.wait_ge(scr_ok[n], WRITES[n])
                    act.activation(qk_h[:, n, :], work(step), ACT.Copy).then_inc(h_ok, 1)
                if kind == "maxrow":
                    wait_filled(act, step)
                    if NTH[step] > 1:
                        pb, pg = GROUP_LIST[NTH[step] - 2]
                        act.wait_ge(st_max[pg], 32 * (pb + 1))
                    act.activation(maxrow[:], work(step)[0:2 * GJ, :], ACT.Copy).then_inc(mrow_ok, 1)
                if kind == "exp":
                    head, half_ = NH * b + n // 2, n % 2
                    if head >= NPROB:
                        pb, pg = GROUP_LIST[(head - NPROB) // GJ]
                        wait_filled(act, ("pv", pb, NT * pg + NT - 1))
                    exps += 1
                    act.wait_ge(exp_filled, exps)
                    act.activation(probs[:, head % NPROB, 2 * half_:2 * half_ + 2, :], ps_exp[(exps - 1) % 2][:],
                                   ACT.Exp).then_inc(exp_ok, 1)
                if kind == "pv" and n % NT == NT - 1:
                    wait_filled(act, step)
                    if NTH[step] > 1:
                        wait_filled(act, ("tr_o", *GROUP_LIST[NTH[step] - 2]))
                    act.activation(o_sb[:], work(step), ACT.Copy).then_inc(o_ok, 1)
                if kind == "tr_attn":
                    wait_filled(act, step)
                    wait_filled(act, ("proj", 1, NT + 1) if b == 0 else ("out", 0, 1))
                    m, dst = ((KA, nt_a), (KB, nt_b))[n]
                    act.activation(dst[:], work(step)[0:m, :], ACT.Copy).then_inc(nt_ok, 1)
                if kind == "up":
                    wait_filled(act, step)
                    if b:
                        wait_filled(act, ("down", 0, 1))
                    act.activation(hid[:, n, :], work(step), ACT.Gelu, bias=col("b1")[:, n:n + 1]).then_inc(hid_ok, 1)

        @block.tensor
        def _(pe):
            ident = col("ident")

            def turn(step, src, m, ok=None, count=0):
                for t in range(NT):
                    if ok is not None:
                        pe.wait_ge(ok, count + t + 1)
                    mm = pe.transpose(work(step)[0:m, P * t:P * (t + 1)], src(t), ident)
                return mm

            def contract(dst, a, b_, tokens, lo, hi):
                pe.matmul(dst, a[:, tokens], wa_sb[:, lo:hi], start=True, stop=False)
                return pe.matmul(dst, b_[:, tokens], wb_sb[:, lo:hi], start=False, stop=True)

            def tile(t):
                return slice(P * t, P * (t + 1))

            pe.wait_ge(const_ok, 1)
            maxs = exps = 0
            for step in STEPS:
                kind, b, n = step
                if kind in FILLING:
                    if BEFORE.get(step):
                        wait_read(pe, BEFORE[step])
                    if step in TAIL and BANK[step] >= 2:
                        pe.wait_ge(*((exp_ok, 2 * NH * B) if BANK[step] < 6 else (max_ok, NT * NH * B)))
                    w = work(step)
                if kind == "gn":
                    if n == 0:
                        pe.wait_ge(x_in[b], 16)
                    else:
                        pe.wait_ge(squared, b + 1)
                    for t in range(NT):
                        mm = pe.matmul(w[:, 0:D], mean_w[:], x_sb[:, b, t, :] if n == 0 else squares[:, t, :],
                                       start=(t == 0), stop=(t == NT - 1))
                if kind in ("norm1", "norm3"):
                    if n == 0:
                        pe.wait_ge(small_in, 16)
                    lo, hi = ((0, KA), (KA, D))[n]
                    mm = turn(step, lambda t: z_sb[:, t, lo:hi], hi - lo, z_ok, NT * (b + (B if kind == "norm3" else 0)))
                if kind == "proj":
                    pe.wait_ge(nt_ok, 2 * b + 2)
                    pe.wait_ge(wq_scaled, 2)
                    if n < NT:
                        mm = contract(w[:, 0:DQK], nt_a, nt_b, tile(n), 0, DQK)
                    else:
                        for k in range(2):
                            mm = contract(w[:, D * k:D * (k + 1)], nt_a, nt_b, tile(2 * (n - NT) + k), DQK, 3 * D)
                if kind == "tr_qk":
                    mm = turn(step, lambda t: qk_sb[:, t, 8 * n:8 * (n + 1), :].rearrange("p h d -> p (h d)"), P,
                              rope_ok, NT * b)
                if kind == "maxrow":
                    pe.wait_ge(split_ok, NTH[step])
                    mm = turn(step, lambda t: negmax_p[:, t].rearrange("p a j -> p (a j)"), 2 * GJ)
                if kind == "max":
                    h, t = divmod(n, NT)
                    pe.wait_ge(st_ok[h], 32 * (b + 1))
                    pe.wait_ge(st_const, 16)
                    pe.wait_ge(st_bias, h + 1)
                    if maxs >= 2:
                        pe.wait_ge(max_ok, maxs - 1)
                    elif 6 + maxs in HEAD_LAST:
                        wait_read(pe, HEAD_LAST[6 + maxs])
                    pe.matmul(ps_max[maxs % 2][:], q_st[0:ROW_MAX, h, tile(t)], k_st[0:ROW_MAX, h, :],
                              start=True, stop=True).then_inc(max_filled, 1)
                    maxs += 1
                if kind == "exp":
                    h, half_ = divmod(n, 2)
                    pe.wait_ge(st_max[h // GJ], 32 * (b + 1))
                    if exps >= 2:
                        pe.wait_ge(exp_ok, exps - 1)
                    else:
                        for k in range(2):
                            if 2 + 2 * exps + k in HEAD_LAST:
                                wait_read(pe, HEAD_LAST[2 + 2 * exps + k])
                    for k in range(2):
                        mm = pe.matmul(ps_exp[exps % 2][:, k, :], k_st[0:ROWS, h, tile(2 * half_ + k)],
                                       q_st[0:ROWS, h, :], start=True, stop=True)
                    mm.then_inc(exp_filled, 1)
                    exps += 1
                if kind == "pv":
                    g, t = divmod(n, NT)
                    pe.wait_ge(proj_ok, (NT + 2) * (b + 1))
                    pe.wait_ge(exp_ok, 2 * (NH * b + GJ * (g + 1)))
                    for j in range(GJ):
                        h = GJ * g + j
                        mm = pe.matmul(w[VW * j:VW * (j + 1), :], v_sb[:, b, t, h, :],
                                       probs[:, (NH * b + h) % NPROB, t, :], start=(t == 0), stop=(t == NT - 1),
                                       tile_position=(0, VW * j))
                if kind == "tr_o":
                    pe.wait_ge(o_ok, NTH[step])
                    mm = turn(step, lambda t: o_sb[:, tile(t)], P)
                if kind == "tr_attn":
                    pe.wait_ge(attn_ok, NG * (b + 1))
                    lo, hi = ((0, KA), (KA, D))[n]
                    mm = turn(step, lambda t: attn[:, t, lo:hi], hi - lo)
                if kind == "out":
                    pe.wait_ge(nt_ok, 2 * B + 2 * (b + 1))
                    for k in range(2):
                        mm = contract(w[:, D * k:D * (k + 1)], nt_a, nt_b, tile(2 * n + k), 3 * D, 4 * D)
                if kind == "up":
                    pe.wait_ge(n3_ok, 2 * (b + 1))
                    lo, hi = 4 * D + P * n, 4 * D + P * (n + 1)
                    pe.matmul(w, wa_sb[:, lo:hi], n3_a[:], start=True, stop=False)
                    mm = pe.matmul(w, wb_sb[:, lo:hi], n3_b[:], start=False, stop=True)
                if kind == "down":
                    pe.wait_ge(w2_in, 16)
                    pe.wait_ge(hid_ok, NF * (b + 1))
                    for k in range(2):
                        for f in range(NF):
                            mm = pe.matmul(w[:, D * k:D * (k + 1)], hid[:, f, tile(2 * n + k)], w2_sb[:, f, :],
                                           start=(f == 0), stop=(f == NF - 1))
                if kind in FILLING and not (kind == "pv" and n % NT < NT - 1):
                    mm.then_inc(filled[BANK[step]], 1)

        @block.vector
        def _(dve):
            links = [0]

            def link(ins):
                links[0] += 1
                ins.then_inc(dve_chain, 1)
                dve.wait_ge(dve_chain, links[0])

            def rsqrt(dst, var, n):
                v, t = newton[:, 0, 0:n], newton[:, 1, 0:n]
                link(dve.tensor_scalar(v, var, EPS, None, ALU.add))
                link(dve.tensor_scalar(t.bitcast(int32), v.bitcast(int32), 1, None, ALU.logical_shift_right))
                link(dve.tensor_scalar(dst.bitcast(int32), t.bitcast(int32), -1.0, float(0x5f3759df), ALU.mult, ALU.add))
                for _ in range(3):
                    link(dve.tensor_tensor(t, dst, dst, ALU.mult))
                    link(dve.scalar_tensor_tensor(out=t, in0=t, scalar=-0.5, in1=v, op0=ALU.mult, op1=ALU.mult))
                    link(dve.scalar_tensor_tensor(out=dst, in0=t, scalar=1.5, in1=dst, op0=ALU.add, op1=ALU.mult))

            def stats(src):
                for t in range(NT):
                    dve.bn_stats(stat[:, t, :], src[:, t, :]).then_inc(dve_chain, 1)
                    links[0] += 1
                for t in range(NT):
                    dve.wait_ge(dve_chain, links[0] - NT + t + 1)
                    dve.bn_aggr(mv[:, t, :], stat[:, t, :]).then_inc(*((stats_ok, 1) if t == NT - 1 else (dve_chain, 1)))
                links[0] += NT - 1

            def normed(src, count):
                dve.wait_ge(rstd_ok, count)
                for t in range(NT):
                    dve.tensor_scalar(z_sb[:, t, :], src[:, t, :], mv[:, t, 0:1], rstd[:, t:t + 1],
                                      ALU.subtract, ALU.mult).then_inc(z_ok, 1)

            dve.wait_ge(small_in, 16)
            r = slice(ROW_BIAS, ROW_MAX)
            link(dve.tensor_scalar(coef[r, 0, :], col("ab0", r), col("ca", r), None, ALU.mult))
            link(dve.scalar_tensor_tensor(out=coef[r, 1, :], in0=col("ab1", r), scalar=col("cb", r),
                                          in1=coef[r, 0, :], op0=ALU.mult, op1=ALU.add))
            link(dve.tensor_copy(coef[r, 2, :].bitcast(fp32r), coef[r, 1, :]))
            link(dve.tensor_scalar(coef[r, 0, :], coef[r, 2, :], col("low", r), None, ALU.mult))
            dve.tensor_tensor(coef[r, 3, :], coef[r, 1, :], coef[r, 0, :], ALU.subtract).then_inc(coef_ok, 1)

            maxs = 0
            for step in STEPS:
                kind, b, n = step
                if kind == "gn" and n == 0:
                    wait_filled(dve, step)
                    link(dve.tensor_reduce(stat_g[:, 0, :], view(work(step), [GW, GROUPS], [1, GW]), AX.X, ALU.add))
                    dve.tensor_tensor(y_sb[:, b], view(x_sb[:, b], [D, NT], [GW, GROUPS], [1, GW]),
                                      view(stat_g[:, 0, :], [0, NT], [1, GROUPS], [0, GW]), ALU.subtract)\
                       .then_inc(centred, 1)
                if kind == "gn" and n == 1:
                    wait_filled(dve, step)
                    dve.tensor_reduce(stat_g[:, 0, :], view(work(step), [GW, GROUPS], [1, GW]), AX.X, ALU.add)\
                       .then_inc(vars_ok, 1)
                    dve.wait_ge(vars_ok, b + 1)
                    if b == 0:
                        rsqrt(stat_g[:, 1, :], stat_g[:, 0, :], GROUPS)
                if kind == "scale":
                    if b:
                        dve.wait_ge(rstd_ok, 2)
                    dve.wait_ge(squared, b + 1)
                    yv = view(y_sb[:, b], [D, NT], [GW, GROUPS], [1, GW])
                    dve.tensor_tensor(yv, yv, view(stat_g[:, 1, :], [0, NT], [1, GROUPS], [0, GW]), ALU.mult)\
                       .then_inc(gn_ok, 1)
                    dve.wait_ge(gn_ok, b + 1)
                    stats(y_sb[:, b])
                if kind == "z1":
                    if b:
                        wait_filled(dve, ("norm1", 0, 1))
                    normed(y_sb[:, b], 1 + 2 * b)
                if kind == "stats3":
                    dve.wait_ge(flat_ok, 2 * b + 2)
                    stats(flat)
                if kind == "z3":
                    wait_filled(dve, ("norm1", 1, 1) if b == 0 else ("norm3", 0, 1))
                    normed(flat, 4 + b)
                if kind == "proj":
                    wait_filled(dve, step)
                    dve.wait_ge(rows_scaled, 1)
                    if n < NT:
                        if b:
                            wait_filled(dve, ("tr_qk", b - 1, 2))
                        dve.tensor_tensor(qk_sb[:, n].rearrange("p h d -> p (h d)"), work(step)[:, 0:DQK],
                                          rows_sb[:, 0:DQK], ALU.add).then_inc(proj_ok, 1)
                        dve.wait_ge(proj_ok, NTH[step])
                        low, high = qk_sb[:, n, :, 0:4], qk_sb[:, n, :, 8:12]
                        both = view(qk_sb[:, n], [HD, 2 * NH], [HD // 2, 2], [1, 4])
                        at = slice(4 * n, 4 * n + 4)
                        dve.tensor_tensor(rot[:], both, view(col("cos")[:, at], [0, 2 * NH], [0, 2], [1, 4]), ALU.mult)\
                           .then_inc(dve_chain, 1)
                        dve.tensor_tensor(rot2[:, :, 0, :], high, view(col("nsin")[:, at], [0, 2 * NH], [1, 4]),
                                          ALU.mult).then_inc(dve_chain, 1)
                        dve.tensor_tensor(rot2[:, :, 1, :], low, view(col("sin")[:, at], [0, 2 * NH], [1, 4]),
                                          ALU.mult).then_inc(dve_chain, 1)
                        links[0] += 3
                        dve.wait_ge(dve_chain, links[0])
                        dve.tensor_tensor(both, rot[:], rot2[:], ALU.add).then_inc(rope_ok, 1)
                        dve.wait_ge(rope_ok, NT * b + n + 1)
                    else:
                        dve.wait_ge(v_ones, 1)
                        t = 2 * (n - NT)
                        for k in range(2):
                            ins = dve.tensor_tensor(v_sb[:, b, t + k, :, 0:HD], view(work(step)[:, D * k:D * (k + 1)],
                                                    [HD, NH], [1, HD]), view(rows_sb[:, DQK:3 * D], [HD, NH], [1, HD]),
                                                    ALU.add)
                            if k == 0:
                                link(ins)
                        ins.then_inc(proj_ok, 1)
                if kind == "tr_qk":
                    dve.wait_ge(h_ok, 3 * b + n + 1)
                    if b:
                        dve.wait_ge(scr_ok[n], WRITES[n])
                    dve.tensor_tensor(qk_l[:, n, :], work(step), qk_h[:, n, :].bitcast(fp32), ALU.subtract)\
                       .then_inc(l_ok, 1)
                if kind == "max":
                    h, t = divmod(n, NT)
                    if n % (GJ * NT) == 0 and maxs:
                        dve.wait_ge(split_ok, NG * b + h // GJ)
                    maxs += 1
                    dve.wait_ge(max_filled, maxs)
                    dve.tensor_reduce(negmax[:, t, h % GJ:h % GJ + 1], ps_max[(maxs - 1) % 2][:], AX.X, ALU.max,
                                      negate=True).then_inc(max_ok, 1)
                if kind == "split":
                    dve.wait_ge(max_ok, maxs)
                    if NTH[step] > 1:
                        wait_filled(dve, ("maxrow", *GROUP_LIST[NTH[step] - 2]))
                    link(dve.tensor_copy(negmax_p[:, :, 0, :].bitcast(fp32r), negmax[:]))
                    dve.tensor_tensor(negmax_p[:, :, 1, :], negmax[:], negmax_p[:, :, 0, :], ALU.subtract)\
                       .then_inc(split_ok, 1)
                if kind == "tr_o":
                    wait_filled(dve, step)
                    if b and n == 0:
                        wait_filled(dve, ("tr_attn", 0, 1))
                    link(dve.reciprocal(rec[:], view(work(step)[:, HD:HD + 1], [P, NT], [VW, GJ])))
                    dve.tensor_tensor(view(attn[:, :, 64 * n:64 * (n + 1)], [D, NT], [HD, GJ], [1, HD]),
                                      view(work(step), [P, NT], [VW, GJ], [1, HD]),
                                      view(rec[:], [GJ, NT], [1, GJ], [0, HD]), ALU.mult).then_inc(attn_ok, 1)
                if kind == "out":
                    wait_filled(dve, step)
                    dve.wait_ge(ybo_ok, b + 1)
                    if b and n == 0:
                        dve.wait_ge(res_ok, b)
                    dve.tensor_tensor(flat[:, 2 * n:2 * n + 2, :], view(work(step), [D, 2], [1, D]),
                                      y_sb[:, b, 2 * n:2 * n + 2, :], ALU.add).then_inc(flat_ok, 1)
                if kind == "down":
                    wait_filled(dve, step)
                    dve.wait_ge(res_ok, b + 1)
                    if b:
                        dve.wait_ge(stored, 16 * 2 * b)
                    dve.tensor_tensor(y_out[:, 2 * n:2 * n + 2, :], view(work(step), [D, 2], [1, D]),
                                      res[:, 2 * n:2 * n + 2, :], ALU.add).then_inc(out_ok, 1)


def kernel(**inputs):
    import numpy as np
    import concourse.bacc as bacc
    from concourse.bass_utils import run_bass_kernel_spmd as run

    p = {k.removeprefix("L0_conv_"): np.asarray(v) for k, v in inputs.items()}
    f = np.float32

    def chunks(v):
        a = np.zeros((P, 2), f)
        a[:, 0] = v[:KA]
        a[:KB, 1] = v[KA:]
        return a

    fraction = f(2.0) * np.arange(4, dtype=f) / f(HD)
    angles = np.arange(T, dtype=f)[:, None] / (f(10000.0) ** fraction).astype(f)[None, :]
    table = {"cos": np.cos(angles), "sin": np.sin(angles), "nsin": -np.sin(angles)}
    table = {k: v.astype(f).reshape(NT, P, 4).transpose(1, 0, 2).reshape(P, NT * 4) for k, v in table.items()}
    row = np.arange(P)
    low = ((row >= ROW_BIAS + C) & (row < ROW_BIAS + 2 * C)) | (row == ROW_BIAS + 2 * C + 1)
    is_b1 = row >= ROW_BIAS + 2 * C
    small = np.concatenate([
        np.eye(P, dtype=f), table["cos"], table["sin"], table["nsin"], chunks(p["ln1_g"]), chunks(p["ln1_b"]),
        chunks(p["ln3_g"]), chunks(p["ln3_b"]), p["b1"].reshape(NF, P).T, low.astype(f)[:, None],
        np.where(is_b1, 0, 1).astype(f)[:, None], np.where(is_b1, 1, -1).astype(f)[:, None],
        np.broadcast_to(p["attn_biases"][:, 0], (P, NH)), np.broadcast_to(p["attn_biases"][:, 1], (P, NH))], axis=1)
    w = np.concatenate([p["wq"], p["wk"], p["wv"], p["wo"], p["w1"]], axis=1)
    onehot = (np.arange(C)[:, None] == np.arange(T)[None, :] // S).astype(f)
    arrays = {
        "x": p["x"], "small": small, "wa": w[:KA], "wb": w[KA:],
        "w2": p["w2"].reshape(NF, P, D).transpose(1, 0, 2),
        "rows": np.concatenate([p[k] for k in ("bq", "bk", "bv", "bo", "b2")]),
        "keyrows": np.concatenate([onehot, onehot, np.ones((ROWS - ROW_BIAS - 2 * C, T), f)]),
    }
    nc = bacc.Bacc("TRN2", target_bir_lowering=False, num_devices=1)
    arrays = {f"in_{k}": np.ascontiguousarray(v) for k, v in arrays.items()}
    args = [nc.dram_tensor(k, v.shape, fp32, kind="ExternalInput").ap() for k, v in arrays.items()]
    out = nc.dram_tensor("out_0", (B, C, S, D), fp32, kind="ExternalOutput").ap()
    build(nc, *args, out)
    return run(nc, [arrays], core_ids=[0]).results[0]["out_0"]
```

```python
import concourse.bass as bass
from concourse import mybir
from contextlib import ExitStack

fp32 = mybir.dt.float32
fp32r = mybir.dt.float32r
int32 = mybir.dt.int32
ALU = mybir.AluOpType
ACT = mybir.ActivationFunctionType
AX = mybir.AxisListType

P = 128
B, C, S, D = 2, 16, 32, 192
T = C * S
NT = T // P
NH, HD = 12, 16
F = 768
NF = F // P
GROUPS, GW = 32, D // 32
GJ = 4
NG = NH // GJ
EPS = 1e-5
KA, KB = P, D - P
DQK = 2 * D

ROW_BIAS, ROW_MAX, ROWS = 64, 98, 100
VW = 32

COL = {}
_at = 0
for _name, _n in (("ident", P), ("cos", NT * 4), ("sin", NT * 4), ("nsin", NT * 4), ("g1", 2), ("c1", 2), ("g3", 2),
                  ("c3", 2), ("b1", NF), ("bv", 2), ("qscale", 1), ("low", 1), ("ca", 1), ("cb", 1),
                  ("ab0", NH), ("ab1", NH)):
    COL[_name] = (_at, _at + _n)
    _at += _n
NSMALL = _at
NW = 3 * D + D + F
NWS = 3 * D + F
NROW = 2 * D + D + D
NPROB = 10
PER = GJ * NT

EXP_LAG = 24
WORK_BANKS, EXP_BANKS, MAX_BANKS = (0, 1), (2, 3, 4), (5, 6, 7)


HEAD = (
    ("sum", 0, 0), ("gn", 0, 0), ("centre", 0, 0), ("sum", 0, 1), ("wsplit", 0, 0),
    ("var", 0, 0), ("swap", 0, 0), ("scale", 0, 0), ("stats1", 0, 0), ("gn", 0, 1),
    ("stats1", 0, 1), ("swap", 0, 1), ("stats1", 0, 2), ("stats1", 0, 3), ("wbias", 0, 0),
    ("z1", 0, 0), ("z1", 0, 1), ("z1", 0, 2), ("sum", 1, 0), ("warm", 0, 0),
    ("wbias", 0, 2), ("z1", 0, 3), ("low1", 0, 0), ("norm1", 0, 0), ("low1", 0, 1),
    ("norm1", 0, 1), ("gn", 1, 0), ("warm", 0, 1), ("centre", 1, 0), ("sum", 1, 1),
    ("direct", 0, 0), ("direct", 0, 1), ("var", 1, 0), ("gn", 1, 1), ("scale", 1, 0),
    ("qbias", 0, 0), ("parts", 0, 0), ("warm", 0, 2), ("proj", 0, 0), ("stack", 0, 0),
    ("stack", 0, 1), ("proj", 0, 1), ("proj", 0, 2), ("warm", 0, 3), ("proj", 0, 3),
)
FILL = (
    (0, ("stack", 0, 2)), (0, ("stack", 0, 3)), (0, ("stack", 0, 4)), (0, ("qbias", 0, 4)),
    (0, ("qbias", 0, 5)), (0, ("stats1", 1, 0)), (1, ("warm", 0, 4)), (3, ("tr_qk", 0, 1)),
    (4, ("warm", 0, 5)), (5, ("wbias", 0, 1)), (6, ("stack", 0, 5)), (6, ("stack", 0, 6)),
    (7, ("stats1", 1, 1)), (7, ("stats1", 1, 2)), (7, ("stats1", 1, 3)), (7, ("proj", 0, 4)),
    (7, ("stack", 0, 7)), (8, ("tr_qk", 0, 2)), (9, ("warm", 0, 6)), (10, ("warm", 0, 7)),
    (11, ("qbias", 0, 7)), (11, ("z1", 1, 0)), (11, ("z1", 1, 1)), (12, ("wbias", 0, 3)),
    (13, ("z1", 1, 2)), (13, ("proj", 0, 5)), (13, ("norm1", 1, 0)), (14, ("z1", 1, 3)),
    (14, ("low1", 1, 0)), (14, ("low1", 1, 1)), (14, ("qbias", 0, 6)), (15, ("norm1", 1, 1)),
    (18, ("qbias", 0, 10)), (18, ("proj", 1, 0)), (19, ("proj", 1, 1)), (21, ("qbias", 0, 9)),
    (22, ("proj", 1, 2)), (25, ("proj", 1, 3)), (25, ("warm", 0, 8)), (27, ("tr_qk", 1, 0)),
    (27, ("qbias", 0, 8)), (29, ("qbias", 0, 11)), (30, ("tr_qk", 1, 1)), (38, ("tr_qk", 1, 2)),
    (42, ("proj", 1, 4)), (47, ("proj", 1, 5)), (51, ("residual", 0, 0)), (53, ("residual", 1, 0)),
    (64, ("wsplit", 0, 1)), (67, ("warm", 0, 9)), (87, ("tr_attn", 0, 0)), (89, ("tr_attn", 0, 1)),
    (91, ("out", 0, 0)), (94, ("out", 0, 1)), (95, ("stats3", 0, 0)), (95, ("stats3", 0, 1)),
    (95, ("stats3", 0, 2)), (99, ("stats3", 0, 3)), (102, ("z3", 0, 0)), (102, ("low3", 0, 0)),
    (102, ("low3", 0, 1)), (103, ("norm3", 0, 0)), (103, ("z3", 0, 1)), (104, ("z3", 0, 2)),
    (104, ("z3", 0, 3)), (107, ("norm3", 0, 1)),
)
TAIL = (
    ("up", 0, 0), ("tr_o", 1, 2), ("up", 0, 1), ("up", 0, 2), ("tr_attn", 1, 0),
    ("tr_attn", 1, 1), ("up", 0, 3), ("out", 1, 0), ("out", 1, 1), ("up", 0, 4),
    ("stats3", 1, 0), ("stats3", 1, 1), ("stats3", 1, 2), ("stats3", 1, 3), ("z3", 1, 0),
    ("z3", 1, 1), ("up", 0, 5), ("z3", 1, 2), ("z3", 1, 3), ("down", 0, 0),
    ("norm3", 1, 0), ("down", 0, 1), ("norm3", 1, 1), ("up", 1, 0), ("low3", 1, 0),
    ("up", 1, 1), ("up", 1, 2), ("up", 1, 3), ("low3", 1, 1), ("up", 1, 4),
    ("up", 1, 5), ("down", 1, 0), ("down", 1, 1),
)
MAXROW_AT, PV_AT, TR_O_AT = 3, 3, (16, 16, 14, 14, 14)


def schedule():
    slots = {}

    def put(k, *steps):
        slots.setdefault(k, []).extend(steps)

    units = NH * NT
    for k in range(B * units):
        b, u = divmod(k, units)
        put(k, ("max", b, u))
        if u % PER == PER - 1:
            put(k, ("split", b, u // PER))
            put(k + MAXROW_AT, ("maxrow", b, u // PER))
        put(EXP_LAG + k, ("exp", b, u))
        if u % GJ == GJ - 1:
            put(EXP_LAG + k + PV_AT, *(("pv", b, u - GJ + 1 + j) for j in range(GJ)))
        if u % PER == PER - 1 and k < B * units - 1:
            put(EXP_LAG + k + TR_O_AT[k // PER], ("tr_o", b, u // PER))
    for k, step in FILL:
        put(k, step)
    return [(k, step) for k in sorted(slots) for step in slots[k]]


SLOTS = schedule()
MIDDLE = [step for _, step in SLOTS]
STEPS = [*HEAD, *MIDDLE, *TAIL]
GROUP_LIST = [(b, g) for b in range(B) for g in range(NG)]
FILLING = ("direct", "wbias", "gn", "norm1", "norm3", "proj", "tr_qk", "stack", "maxrow", "pv", "tr_o", "tr_attn", "out",
           "up", "down")


def banks():
    bank, turn, before, last, given = {}, {}, {}, {}, {}
    free, n = tuple(range(8)), 0
    after_max = STEPS.index(("max", B - 1, NH * NT - 1))
    for at, step in enumerate(STEPS):
        kind, b, i = step
        if step == MIDDLE[0]:
            free = WORK_BANKS + EXP_BANKS
            given |= {k: last.get(k) for k in MAX_BANKS}
        elif step == ("exp", 0, 0):
            free = WORK_BANKS
            given |= {k: last.get(k) for k in EXP_BANKS}
        elif at == after_max + 1:
            free = free + MAX_BANKS
        elif step == TAIL[0]:
            free = tuple(range(8))
        if kind not in FILLING:
            continue
        if kind == "pv" and i % PER:
            for table in (bank, turn):
                table[step] = table[(kind, b, i - 1)]
            continue
        if kind == "pv":
            group = NG * b + i // PER
            k = WORK_BANKS[group % 2]
            free = WORK_BANKS[(group + 1) % 2:][:1] + tuple(f for f in free if f not in WORK_BANKS)
        else:
            k = free[n % len(free)]
            n += 1
        bank[step] = k
        before[step] = last.get(k)
        turn[step] = turn[last[k]] + 1 if k in last else 1
        last[k] = step
    return bank, turn, before, given, set(STEPS[after_max:])


BANK, TURN, BEFORE, GIVEN, AFTER_MAX = banks()
LATER = {"act": {"proj": 1, "norm1": 2, "tr_qk": 1, "maxrow": 0, "pv": 0, "tr_attn": 1, "norm3": 1, "stack": 2},
         "dve": {"tr_qk": 2, "low1": 2, "low3": 3, "tr_o": 1, "out": 1}}
SLOT_OF = {step: k for k, step in SLOTS}
NEXT = {before: step for step, before in BEFORE.items()}


def order(engine):
    def at(slot_step):
        slot, step = slot_step
        product = (step[0].replace("low", "norm"), *step[1:])
        limit = SLOT_OF.get(NEXT.get(product), slot + 9)
        later = LATER[engine].get(step[0], 0) + (step[0] == "proj" and step[2] >= NT)
        return max(slot, min(slot + later, limit))
    return [*HEAD, *(step for _, step in sorted(SLOTS, key=at)), *TAIL]


LOAD_AFTER = {}
for _b, _g in ((_b, _g) for _b in range(B) for _g in range(NG) if _b or _g):
    _need = [("tr_qk", _b, _g), ("exp", 0, PER * _g + PER - 1) if _b else ("maxrow", 0, 0) if _g == 2 else STEPS[0]]
    LOAD_AFTER.setdefault(max(_need, key=STEPS.index), []).append((_b, _g))
NTH = {}
for _s in STEPS:
    NTH[_s] = 1 + sum(1 for t in NTH if t[0] == _s[0])
for _s in STEPS:
    if _s[0] == "tr_qk":
        NTH[_s] += 1
    if _s[0] == "pv":
        NTH[_s] = NG * _s[1] + _s[2] // PER + 1


def build(nc, x, small, wa, wb, w2, rows, keyrows, table, out):
    ctx = ExitStack()
    with ctx:
        def sb(name, shape, dt=fp32):
            return ctx.enter_context(nc.sbuf_tensor(name, shape, dt))

        def sem(name):
            return ctx.enter_context(nc.semaphore(name))

        def view(ap, *dims):
            return bass.AP(tensor=ap.tensor, offset=ap.offset, ap=[list(ap.ap[0]), *[list(d) for d in dims]])

        x_sb = sb("x_sb", [P, B, NT, D])
        y_sb = sb("y_sb", [P, B, NT, D])
        small_sb = sb("small_sb", [P, NSMALL])
        wa_sb = sb("wa_sb", [KA, NW])
        wb_sb = sb("wb_sb", [P, NW])
        wa_h = sb("wa_h", [KA, NWS], fp32r)
        wa_l = sb("wa_l", [KA, NWS], fp32r)
        wb_h = sb("wb_h", [P, NWS], fp32r)
        wb_l = sb("wb_l", [P, NWS], fp32r)
        w2_sb = sb("w2_sb", [P, NF, D])
        rows_sb = sb("rows_sb", [P, NROW])
        keyrows_sb = sb("keyrows_sb", [P, T])
        mean_w = sb("mean_w", [P, P])
        squares = sb("squares", [P, NT, D])
        y_out = squares
        sums = sb("sums", [P, 2, GROUPS])
        z_sb = sb("z_sb", [P, NT, D])
        n1 = [sb(f"n1_{k}", [P, T], fp32r) for k in ("high", "low", "rest")]
        n3 = [sb(f"n3_{k}", [P, T], fp32r) for k in ("high", "low", "rest")]
        at_a, at_b = wa_sb[:, 0:T], wb_sb[0:KB, 0:T]
        qk_sb = sb("qk_sb", [P, NT, 2 * NH, HD])
        rot = sb("rot", [P, 2, 2, 2 * NH, 2, 4])
        v_sb = sb("v_sb", [P, B, NT, NH, VW])
        qk_h = sb("qk_h", [P, 3, T], fp32r)
        qk_l = sb("qk_l", [P, 3, T], fp32r)
        q_st = sb("q_st", [P, NH, T], fp32r)
        k_st = sb("k_st", [P, NH, T], fp32r)
        probs = sb("probs", [P, NPROB, T])
        negmax = sb("negmax", [P, NT, GJ])
        negmax_p = sb("negmax_p", [P, NT, 2, GJ])
        maxrow = sb("maxrow", [2 * GJ, T], fp32r)
        o_sb = keyrows_sb
        b1_sb = sb("b1_sb", [P, NF])
        bv_sb = sb("bv_sb", [P, 2])
        bias_p = sb("bias_p", [2 * 32, DQK], fp32r)
        share = sb("share", [2 * 32, P], fp32r)
        sq = sb("sq", [P, GROUPS])
        rec = sb("rec", [P, NT, GJ])
        spare = qk_sb[:, :, :, :].rearrange("p t h d -> p (t h d)").rearrange("p (a t c) -> p a t c", a=2, t=NT)
        attn, flat = spare[:, 0], spare[:, 1]
        hid_sb = sb("hid_sb", [P, B, NF, T])
        cos_t, sin_t, turned, turned2 = (hid_sb[:, 0, k] for k in range(4))
        swapped = [n3[2][:, P * j:P * (j + 1)] for j in range(4)]
        bias_s = sb("bias_s", [2 * 32, P], fp32r)
        scaled = view(hid_sb[:, B - 1, 0], [F, 2], [1, F])
        sel = n3[0:2]
        stat_g = sb("stat_g", [P, 2, GROUPS])
        stat = sb("stat", [P, NT, 6])
        mv = sb("mv", [P, NT, 2])
        newton = sb("newton", [P, 2, GROUPS])
        rstd = sb("rstd", [P, NT])
        shift = sb("shift", [P, 2, NT])
        pool_v = sb("pool_v", [P, GROUPS])
        half = sb("half", [P, GROUPS])
        coef = sb("coef", [P, 4, NH])

        ps = [ctx.enter_context(nc.psum_tensor(f"bank{i}", [P, T], fp32))[:, :] for i in range(8)]
        scr = nc.dram_tensor("qk_scratch", (B, NG, 2 * GJ, 3 * HD, T), fp32, kind="Internal").ap()

        x_in = [sem(f"x_in{k}") for k in range(3)]
        small_in = sem("small_in")
        key_in = sem("key_in")
        wa_in = sem("wa_in")
        wb_in = sem("wb_in")
        w2_in = sem("w2_in")
        rows_in = sem("rows_in")
        filled = [sem(f"filled{i}") for i in range(8)]
        const_ok = sem("const_ok")
        v_ones = sem("v_ones")
        centred = sem("centred")
        stats_ok = sem("stats_ok")
        rstd_ok = sem("rstd_ok")
        eps_ok = sem("eps_ok")
        squared = sem("squared")
        vars_ok = sem("vars_ok")
        gn_ok = sem("gn_ok")
        z_ok = sem("z_ok")
        n1h_ok = sem("n1h_ok")
        n1l_ok = sem("n1l_ok")
        n3h_ok = sem("n3h_ok")
        n3l_ok = sem("n3l_ok")
        at_ok = sem("at_ok")
        wh_ok = [sem(f"wh_ok{i}") for i in range(2)]
        wl_ok = [sem(f"wl_ok{i}") for i in range(2)]
        w_scaled = sem("w_scaled")
        wbias_ok = sem("wbias_ok")
        summed = sem("summed")
        std_ok = sem("std_ok")
        proj_ok = sem("proj_ok")
        rope_ok = [sem(f"rope_ok{t}") for t in range(NT)]
        h_ok = sem("h_ok")
        l_ok = sem("l_ok")
        scr_ok = [sem(f"scr_ok{c}") for c in range(3)]
        st_ok = [sem(f"st_ok{g}") for g in range(NG)]
        st_const = sem("st_const")
        st_bias = sem("st_bias")
        coef_ok = sem("coef_ok")
        max_filled = sem("max_filled")
        max_ok = sem("max_ok")
        split_ok = sem("split_ok")
        mrow_ok = sem("mrow_ok")
        st_max = [sem(f"st_max{g}") for g in range(NG)]
        exp_filled = sem("exp_filled")
        exp_ok = sem("exp_ok")
        o_ok = sem("o_ok")
        attn_ok = sem("attn_ok")
        flat_ok = sem("flat_ok")
        ybo_ok = sem("ybo_ok")
        xb2_ok = sem("xb2_ok")
        res_ok = sem("res_ok")
        hid_ok = sem("hid_ok")
        out_ok = sem("out_ok")
        stored = sem("stored")
        pool_v_ok = sem("pool_v_ok")
        rot_ok = [sem(f"rot_ok{e}") for e in range(2)]
        bias_ok = sem("bias_ok")
        table_in = sem("table_in")
        swap_ok = sem("swap_ok")
        direct_ok = sem("direct_ok")
        shift_ok = sem("shift_ok")
        sel_ok = sem("sel_ok")
        stacked = sem("stacked")
        pv_used = sem("pv_used")
        dve_chain = sem("dve_chain")
        block = ctx.enter_context(nc.Block())

        read = {"direct": direct_ok, "wbias": wbias_ok, "norm1": n1l_ok, "tr_attn": at_ok, "norm3": n3l_ok, "proj": proj_ok, "tr_qk": l_ok,
                "stack": stacked,
                "maxrow": mrow_ok, "pv": o_ok, "tr_o": attn_ok, "out": flat_ok, "up": hid_ok, "down": out_ok}

        def wait_read(eng, step):
            kind, b, n = step
            if kind == "gn":
                eng.wait_ge((centred, vars_ok)[n], (2, 1)[n] * (b + 1))
            else:
                eng.wait_ge(read[kind], NTH[step])

        def wait_filled(eng, step):
            eng.wait_ge(filled[BANK[step]], TURN[step])

        def col(name, rows_=slice(None)):
            return small_sb[rows_, COL[name][0]:COL[name][1]]

        def work(step):
            return ps[BANK[step]]

        WRITES = 48

        FIRST = (P, 0)
        ROPES = ([(0, 0), (0, 1), (0, 2), (1, 3)], [(0, 3), (1, 0), (1, 1), (1, 2)])

        def rope(eng, e, b, n):
            times = ROPES[e].index((b, n))
            before = ROPES[e][times - 1] if times else None
            eng.wait_ge(proj_ok, (NT + 2) * b + n + 1)
            first = FIRST[b] // HD
            heads = 2 * NH - first
            low, high = qk_sb[:, n, first:, 0:4], qk_sb[:, n, first:, 8:12]
            both = view(qk_sb[:, n, first], [HD, heads], [HD // 2, 2], [1, 4])
            own, partner = rot[:, e, 0, first:], rot[:, e, 1, first:]
            at = slice(4 * n, 4 * n + 4)
            if before:
                eng.wait_ge(rope_ok[before[1]], before[0] + 1)
            eng.tensor_tensor(own, both, view(col("cos")[:, at], [0, heads], [0, 2], [1, 4]), ALU.mult)\
               .then_inc(rot_ok[e], 1)
            eng.tensor_tensor(partner[:, :, 0, :], high, view(col("nsin")[:, at], [0, heads], [1, 4]), ALU.mult)\
               .then_inc(rot_ok[e], 1)
            eng.tensor_tensor(partner[:, :, 1, :], low, view(col("sin")[:, at], [0, heads], [1, 4]), ALU.mult)\
               .then_inc(rot_ok[e], 1)
            eng.wait_ge(rot_ok[e], 3 * (times + 1))
            eng.tensor_tensor(both, own, partner, ALU.add).then_inc(rope_ok[n], 1)

        def wait_stacks(eng, b, h):
            if b == 0 and h < GJ:
                eng.wait_ge(stacked, 2 * (h + 1))
            else:
                eng.wait_ge(st_ok[h // GJ], 64 * (b + (h >= GJ)))

        def wait_pv(eng, i):
            g, u = divmod(i, PER)
            if u == PER - 1:
                wait_filled(eng, ("pv", g // NG, PER * (g % NG) + u))
            else:
                eng.wait_ge(pv_used, (PER - 1) * g + u + 1)

        PIECES = ((0, 3 * D, 0, col("g1")), (4 * D, 4 * D + F, 3 * D, col("g3")))

        def scale(eng, b):
            eng.wait_ge(squared, 2 * (b + 1))
            if b:
                eng.wait_ge(rstd_ok, 2)
            yv = view(y_sb[:, b], [D, NT], [GW, GROUPS], [1, GW])
            eng.tensor_tensor(yv, yv, view(stat_g[:, 1, :], [0, NT], [1, GROUPS], [0, GW]), ALU.mult)\
               .then_inc(gn_ok, 1)

        @block.sync
        def _(sp):
            tokens = "b (v c) s d -> b (c s) v d"
            xv, ov = x.rearrange(tokens, v=NT), out.rearrange(tokens, v=NT)
            for half_ in range(2):
                tiles = slice(2 * half_, 2 * half_ + 2)
                sp.dma_start(x_sb[:, 0, tiles], xv[0][:, tiles]).then_inc(x_in[half_], 16)
            sp.dma_start(wa_sb[:], wa).then_inc(wa_in, 16)
            for half_ in range(2):
                sp.dma_start(wb_sb[KB * half_:KB * (half_ + 1), :], wb).then_inc(wb_in, 16)
            sp.dma_start(rows_sb[:], rows.partition_broadcast(P)).then_inc(rows_in, 16)
            sp.dma_start(view(cos_t, [1, 2 * T]), table).then_inc(table_in, 16)
            sp.dma_start(x_sb[:, 1], xv[1]).then_inc(x_in[2], 16)
            sp.dma_start(keyrows_sb[ROW_BIAS:ROWS, :], keyrows).then_inc(key_in, 16)
            sp.dma_start(w2_sb[:], w2).then_inc(w2_in, 16)
            sp.wait_ge(key_in, 16)
            sp.dma_start(k_st[ROW_BIAS:ROWS, :, :].bitcast(fp32),
                         view(keyrows_sb[ROW_BIAS:ROWS, :], [0, NH], [1, T])).then_inc(st_const, 16)

            def load_group(b, g):
                sp.wait_ge(scr_ok[g], WRITES * (b + (g > 0)))
                if b:
                    sp.wait_ge(exp_ok, PER * (g + 1))
                for st, at, starts in ((q_st, 0, (1, 1)), (k_st, GJ, (0, 1))):
                    for k, start in enumerate(starts):
                        src = scr[b, g, at:at + GJ, HD * start:HD * (start + 2), :].rearrange("h r t -> r h t")
                        sp.dma_start(st[32 * k:32 * (k + 1), GJ * g:GJ * (g + 1), :].bitcast(fp32), src)\
                            .then_inc(st_ok[g], 16)

            for step in STEPS:
                kind, b, n = step
                if kind == "tr_qk" and (b or n):
                    for src, ok, row, first in ((qk_h, h_ok, 1, 0), (qk_l, l_ok, 2, 0), (qk_l, l_ok, 0, GJ)):
                        sp.wait_ge(ok, NG * b + n + 1)
                        sp.dma_start(scr[b, n, first:, HD * row:HD * (row + 1), :],
                                     src[HD * first:P, n, :].bitcast(fp32)).then_inc(scr_ok[n], 16)
                for lb, lg in LOAD_AFTER.get(step, []):
                    load_group(lb, lg)
                if kind == "maxrow":
                    sp.wait_ge(mrow_ok, NG * b + n + 1)
                    for part in range(2):
                        dst = q_st[ROW_MAX + part:ROW_MAX + part + 1, GJ * n:GJ * (n + 1), :].bitcast(fp32)
                        sp.dma_start(dst, maxrow[GJ * part:GJ * (part + 1), :].bitcast(fp32)).then_inc(st_max[n], 16)
                if kind == "down":
                    sp.wait_ge(out_ok, 2 * b + n + 1)
                    sp.dma_start(ov[b][:, 2 * n:2 * n + 2], y_out[:, 2 * n:2 * n + 2, :]).then_inc(stored, 16)
            sp.wait_ge(stored, 16 * 2 * B)

        @block.gpsimd
        def _(pool):
            pool.memset(mean_w[:], 1.0 / (T * GW)).then_inc(const_ok, 1)
            pool.memset(share[:].bitcast(fp32), 1.0 / 32).then_inc(const_ok, 1)
            pool.memset(v_sb[:], 1.0).then_inc(v_ones, 1)
            pool.memset(half[:], -0.5).then_inc(eps_ok, 1)

            def weights_low(which):
                lo, hi, at, gain = PIECES[which]
                chunks = ((wa_sb, wa_h, wa_l), (wb_sb, wb_h, wb_l))
                for c, (w, high, dst) in enumerate(chunks):
                    pool.wait_ge(*((wa_in, 16), (wb_in, 32))[c])
                    if which:
                        pool.wait_ge(wl_ok[0], c + 1)
                    pool.tensor_scalar(scaled[:, c, 0:hi - lo], w[:, lo:hi], gain[:, c:c + 1], None, ALU.mult)\
                        .then_inc(w_scaled, 1)
                for c, (w, high, dst) in enumerate(chunks):
                    pool.wait_ge(w_scaled, 2 * which + c + 1)
                    pool.wait_ge(wh_ok[which], c + 1)
                    pool.tensor_tensor(dst[:, at:at + hi - lo], scaled[:, c, 0:hi - lo],
                                       high[:, at:at + hi - lo].bitcast(fp32), ALU.subtract).then_inc(wl_ok[which], 1)

            def selections():
                for part in range(2):
                    pool.memset(sel[part][:].bitcast(fp32), 0.0).then_inc(sel_ok, 1)
                pool.wait_ge(sel_ok, 2)
                for part, k, first, apart, times in ((0, 0, 0, 2, 2), (1, 0, 1, 2, 2), (0, 1, 1, 1, 2), (1, 1, 0, 3, 2)):
                    dst = view(sel[part][:, 64 * k + HD * first:], [2 * 64, GJ], [HD * apart, times], [1, HD])
                    src = view(col("ident")[:, GJ * HD * k:], [HD, GJ], [0, times], [1, HD])
                    pool.tensor_copy(dst, src).then_inc(sel_ok, 1)

            rstds = 0

            def rsqrt(dst, var, n):
                v = pool_v[:, 0:n]
                pool.tensor_scalar(v, var, EPS, None, ALU.add).then_inc(pool_v_ok, 1)
                pool.wait_ge(pool_v_ok, rstds + 1)
                pool.tensor_tensor(dst, v, half[:, 0:n], ALU.pow).then_inc(rstd_ok, 1)
                pool.wait_ge(rstd_ok, rstds + 1)

            pool.wait_ge(small_in, 16)
            pool.wait_ge(eps_ok, 1)
            for step in STEPS:
                kind, b, n = step
                if step == ("var", 1, 0):
                    pool.wait_ge(vars_ok, b + 1)
                    rsqrt(stat_g[:, 1, :], stat_g[:, 0, :], GROUPS)
                    rstds += 1
                if step == ("scale", 1, 0):
                    scale(pool, b)
                if step == ("wsplit", 0, 1):
                    weights_low(1)
                if step == ("wsplit", 0, 0):
                    weights_low(0)
                if step == ("z1", 0, 0):
                    selections()
                if kind == "proj" and (b, n) in ROPES[1]:
                    rope(pool, 1, b, n)
                if kind in ("stats1", "stats3") and n == NT - 1:
                    pool.wait_ge(stats_ok, b + 1 + (B if kind == "stats3" else 0))
                    rsqrt(rstd[:], mv[:, :, 1], NT)
                    rstds += 1
                    if step == ("stats1", 1, NT - 1):
                        pool.tensor_scalar(shift[:, 0, :], mv[:, :, 0], -1.0, None, ALU.mult).then_inc(shift_ok, 1)
                        pool.wait_ge(shift_ok, 1)
                        pool.tensor_tensor(shift[:, 1, :], shift[:, 0, :], rstd[:], ALU.mult).then_inc(shift_ok, 1)
                if kind == "residual":
                    if b == 0:
                        pool.wait_ge(rows_in, 16)
                    pool.wait_ge(centred, 2 * (b + 1))
                    b2r = view(rows_sb[:, NROW - D:NROW], [0, NT], [1, D])
                    pool.tensor_tensor(x_sb[:, b], x_sb[:, b], b2r, ALU.add).then_inc(xb2_ok, 1)
                    pool.wait_ge(z_ok, NT * (b + 1))
                    pool.wait_ge(wbias_ok, 4)
                    bor = view(rows_sb[:, DQK:3 * D], [0, NT], [1, D])
                    pool.tensor_tensor(y_sb[:, b], y_sb[:, b], bor, ALU.add).then_inc(ybo_ok, 1)
                if kind == "z3" and n == 0:
                    pool.wait_ge(flat_ok, 2 * b + 2)
                    pool.wait_ge(xb2_ok, b + 1)
                    pool.tensor_tensor(x_sb[:, b], flat, x_sb[:, b], ALU.add).then_inc(res_ok, 1)

        @block.scalar
        def _(act):
            act.dma_start(small_sb[:], small).then_inc(small_in, 16)

            def weights_high(which, c):
                lo, hi, at, gain = PIECES[which]
                w, dst = ((wa_sb, wa_h), (wb_sb, wb_h))[c]
                act.activation(dst[:, at:at + hi - lo], w[:, lo:hi], ACT.Copy, scale=gain[:, c:c + 1])\
                   .then_inc(wh_ok[which], 1)

            act.wait_ge(small_in, 16)
            act.wait_ge(const_ok, 1)
            act.activation(sq[:, 0:1], mean_w[:, 0:1], ACT.Sqrt).then_inc(std_ok, 1)
            exps = 0
            for step in order("act"):
                kind, b, n = step
                if kind == "centre":
                    for k in range(2):
                        act.wait_ge(centred, 2 * b + k + 1)
                        if b:
                            act.wait_ge(summed, 4)
                        act.activation(squares[:, 2 * k:2 * k + 2], y_sb[:, b, 2 * k:2 * k + 2], ACT.Square)\
                           .then_inc(squared, 1)
                if step == ("centre", 0, 0):
                    act.wait_ge(wa_in, 16)
                    weights_high(0, 0)
                if step == ("var", 0, 0):
                    act.wait_ge(vars_ok, 1)
                    act.wait_ge(std_ok, 1)
                    act.activation(sq[:], newton[:, 0, :], ACT.Sqrt).then_inc(std_ok, 1)
                    act.wait_ge(wb_in, 32)
                    weights_high(0, 1)
                if kind == "swap":
                    act.wait_ge(*((wl_ok[0], 2), (bias_ok, 1))[n])
                    sources = ((wa_h, wa_l, wb_h, wb_l), (bias_p,))[n]
                    for src, dst in zip(sources, (swapped, [bias_s[:]])[n]):
                        for k in range(2):
                            act.activation(view(dst[:, 8 * k:], [HD, 2 * GJ], [1, 8]),
                                           view(src[:, 8 - 8 * k:].bitcast(fp32), [HD, 2 * GJ], [1, 8]), ACT.Copy)\
                               .then_inc(swap_ok, 1)
                if kind == "parts":
                    act.wait_ge(direct_ok, 3)
                    act.activation(qk_h[:, 0, :], turned, ACT.Copy, scale=col("qscale")).then_inc(h_ok, 1)
                if kind == "qbias":
                    act.wait_ge(coef_ok, 1)
                    act.wait_ge(key_in, 16)
                    for h in range(GJ) if n == 0 else (n,):
                        act.activation(q_st[ROW_BIAS:ROW_MAX, h, :], keyrows_sb[ROW_BIAS:ROW_MAX, :], ACT.Copy,
                                       scale=coef[ROW_BIAS:ROW_MAX, 3, h:h + 1]).then_inc(st_bias, 1)
                if step == ("wsplit", 0, 1):
                    for c in range(2):
                        weights_high(1, c)
                if kind in ("norm1", "norm3"):
                    wait_filled(act, step)
                    if b:
                        wait_filled(act, ("proj", 0, NT + 1) if kind == "norm1" else ("up", 0, NF - 1))
                    elif kind == "norm3":
                        wait_filled(act, ("stack", 0, 2 * GJ - 1))
                    m, dst = ((KA, (n1, n3)[kind == "norm3"][0]), (KB, (n1, n3)[kind == "norm3"][2]))[n]
                    act.activation(dst[0:m, :], work(step)[0:m, :], ACT.Copy)\
                       .then_inc(n1h_ok if kind == "norm1" else n3h_ok, 1)
                if kind == "z1" and b == 1:
                    if n == 0:
                        act.wait_ge(shift_ok, 2)
                        wait_filled(act, ("norm1", 0, 1))
                    act.activation(z_sb[:, n, :], y_sb[:, b, n, :], ACT.Identity, bias=shift[:, 1, n:n + 1],
                                   scale=rstd[:, n:n + 1]).then_inc(z_ok, 1)
                if kind == "proj":
                    wait_filled(act, step)
                    if n < NT:
                        if b:
                            wait_filled(act, ("tr_qk", b - 1, 2))
                        act.activation(qk_sb[:, n].rearrange("p h d -> p (h d)")[:, FIRST[b]:],
                                       work(step)[:, FIRST[b]:DQK], ACT.Copy)\
                           .then_inc(proj_ok, 1)
                    else:
                        act.wait_ge(v_ones, 1)
                        t = 2 * (n - NT)
                        act.activation(v_sb[:, b, t:t + 2, :, 0:HD], view(work(step), [D, 2], [HD, NH], [1, HD]),
                                       ACT.Copy).then_inc(proj_ok, 1)
                if kind == "tr_qk":
                    wait_filled(act, step)
                    if b and n:
                        act.wait_ge(scr_ok[n], WRITES)
                    elif b:
                        wait_filled(act, ("stack", 0, 2 * GJ - 1))
                    act.activation(qk_h[:, n, :], work(step), ACT.Copy, scale=col("qscale")).then_inc(h_ok, 1)
                if kind == "stack":
                    wait_filled(act, step)
                    act.activation((q_st, k_st)[n % 2][0:ROW_BIAS, n // 2, :], work(step)[0:ROW_BIAS, :], ACT.Copy)\
                       .then_inc(stacked, 1)
                if kind == "maxrow":
                    wait_filled(act, step)
                    if NTH[step] > 1:
                        pb, pg = GROUP_LIST[NTH[step] - 2]
                        act.wait_ge(st_max[pg], 32 * (pb + 1))
                    act.activation(maxrow[:], work(step)[0:2 * GJ, :], ACT.Copy).then_inc(mrow_ok, 1)
                if kind == "exp":
                    if exps >= NPROB:
                        wait_pv(act, exps - NPROB)
                    act.wait_ge(exp_filled, exps + 1)
                    act.activation(probs[:, exps % NPROB, :], ps[EXP_BANKS[exps % len(EXP_BANKS)]], ACT.Exp).then_inc(exp_ok, 1)
                    exps += 1
                if kind == "pv" and n % PER == PER - 1:
                    wait_filled(act, step)
                    if NTH[step] > 1:
                        wait_filled(act, ("tr_o", *GROUP_LIST[NTH[step] - 2]))
                    act.wait_ge(st_const, 16)
                    act.activation(o_sb[:], work(step), ACT.Copy).then_inc(o_ok, 1)
                if kind == "tr_attn":
                    wait_filled(act, step)
                    if b:
                        wait_filled(act, ("out", 0, 1))
                    m, dst = ((KA, at_a), (KB, at_b))[n]
                    act.wait_ge(wl_ok[0], 2)
                    act.wait_ge(wbias_ok, 4)
                    act.activation(dst, work(step)[0:m, :], ACT.Copy).then_inc(at_ok, 1)
                if kind == "up":
                    wait_filled(act, step)
                    act.wait_ge(wbias_ok, 4)
                    act.activation(hid_sb[:, b, n, :], work(step), ACT.Gelu, bias=b1_sb[:, n:n + 1]).then_inc(hid_ok, 1)

        @block.tensor
        def _(pe):
            ident = col("ident")

            def turn(step, src, m, ok=None, count=0):
                for t in range(NT):
                    if ok is rope_ok:
                        pe.wait_ge(rope_ok[t], count + 1)
                    elif ok is not None:
                        pe.wait_ge(ok, count + t + 1)
                    mm = pe.transpose(work(step)[0:m, P * t:P * (t + 1)], src(t), ident)
                return mm

            def contract(dst, left, right, more=False):
                pairs = ((0, 0), (0, 1), (1, 0), (2, 2), (2, 3))
                for k, (i, j) in enumerate(pairs):
                    mm = pe.matmul(dst, left(i), right(j), start=(k == 0), stop=(k == len(pairs) - 1 and not more))
                return mm

            def weights(lo, hi):
                return lambda j: (wa_h, wa_l, wb_h, wb_l)[j][:, lo:hi]

            def tile(t):
                return slice(P * t, P * (t + 1))

            pe.wait_ge(const_ok, 1)
            maxs = exps = 0
            taken_back = []

            def wait_max_bank():
                bank = MAX_BANKS[maxs % len(MAX_BANKS)]
                if maxs >= len(MAX_BANKS):
                    pe.wait_ge(max_ok, maxs + 1 - len(MAX_BANKS))
                elif GIVEN[bank]:
                    wait_read(pe, GIVEN[bank])

            for at, step in enumerate(STEPS):
                kind, b, n = step
                if kind in FILLING:
                    if BEFORE.get(step):
                        wait_read(pe, BEFORE[step])
                    if step in AFTER_MAX and BANK[step] in EXP_BANKS + MAX_BANKS and not BANK[step] in taken_back:
                        taken_back.append(BANK[step])
                        pe.wait_ge(exp_ok if BANK[step] in EXP_BANKS else max_ok, NT * NH * B)
                    w = work(step)
                if kind == "warm":
                    following = next((s for s in HEAD[at:] if s in BANK), None)
                    if following is None:
                        wait_max_bank()
                        bank = MAX_BANKS[maxs % len(MAX_BANKS)]
                    else:
                        if BEFORE[following]:
                            wait_read(pe, BEFORE[following])
                        bank = BANK[following]
                    pe.matmul(ps[bank][:, 0:2 * P], mean_w[:], view(mean_w[:], [0, 2], [1, P]), start=True, stop=True)
                if kind == "wbias":
                    pe.wait_ge(small_in, 16)
                    pe.wait_ge(wa_in, 16)
                    pe.wait_ge(wb_in, 32)
                    if n in (0, 3):
                        if n == 3:
                            pe.wait_ge(wbias_ok, NTH[("wbias", 0, 1)])
                        shifts = (col("c1"), bv_sb)[n == 3]
                        lo, hi = ((0, DQK), (3 * D, 4 * D))[n == 3]
                        for c, (wt, m) in enumerate(((wa_sb, KA), (wb_sb, KB))):
                            mm = pe.matmul(w[:, 0:hi - lo], view(shifts[0:m, c:c + 1], [0, P]), wt[0:m, lo:hi],
                                           start=(c == 0), stop=(c == 1))
                    else:
                        shifts = col(("c1", "c3")[n == 2])
                        parts = ((DQK, KA), (DQK + KA, KB)) if n == 1 else [(4 * D + P * j, P) for j in range(NF)]
                        for j, (lo, width) in enumerate(parts):
                            for c, (wt, m) in enumerate(((wa_sb, KA), (wb_sb, KB))):
                                mm = pe.matmul(w[0:width, j:j + 1], wt[0:m, lo:lo + width], shifts[0:m, c:c + 1],
                                               start=(c == 0), stop=(c == 1))
                if kind == "gn":
                    for k in range(2):
                        pe.wait_ge(summed, 4 * b + 2 * n + k + 1)
                        mm = pe.matmul(w[:, 0:GROUPS], mean_w[:], sums[:, k], start=(k == 0), stop=(k == 1))
                if kind in ("norm1", "norm3"):
                    if n == 0:
                        pe.wait_ge(small_in, 16)
                    lo, hi = ((0, KA), (KA, D))[n]
                    mm = turn(step, lambda t: z_sb[:, t, lo:hi], hi - lo, z_ok, NT * (b + (B if kind == "norm3" else 0)))
                if kind == "direct":
                    if n == 0:
                        pe.wait_ge(n1l_ok, 2)
                        pe.wait_ge(wl_ok[0], 2)
                        pe.wait_ge(bias_ok, 1)
                        pe.wait_ge(const_ok, 2)
                    else:
                        pe.wait_ge(swap_ok, 10)
                    left = weights(0, P) if n == 0 else lambda j: swapped[j]
                    for k, (i, j) in enumerate(((0, 0), (1, 0), (0, 1), (2, 2), (3, 2))):
                        pe.matmul(w, left(i), n1[j][:], start=(k == 0), stop=False)
                    mm = pe.matmul(w, (bias_p[:, 0:P], bias_s[:])[n], view(share[:, 0:1], [0, T]), start=False, stop=True)
                if kind == "proj":
                    if n == 0:
                        pe.wait_ge(n1l_ok, 2 * b + 2)
                        pe.wait_ge(wl_ok[0], 2)
                        pe.wait_ge(bias_ok, 1)
                        pe.wait_ge(const_ok, 2)
                    if n < NT:
                        lo = FIRST[b]
                        contract(w[:, lo:DQK], lambda i: n1[i][:, tile(n)], weights(lo, DQK), more=True)
                        mm = pe.matmul(w[:, lo:DQK], share[:], bias_p[:, lo:], start=False, stop=True)
                    else:
                        for k in range(2):
                            mm = contract(w[:, D * k:D * (k + 1)], lambda i: n1[i][:, tile(2 * (n - NT) + k)],
                                          weights(DQK, 3 * D))
                if kind == "stack":
                    if n == 0:
                        pe.wait_ge(sel_ok, 6)
                        pe.wait_ge(l_ok, 1)
                    for part, src in enumerate((qk_h, qk_l)):
                        mm = pe.matmul(w[0:ROW_BIAS, :], sel[part][:, 64 * n:64 * (n + 1)], src[:, 0, :],
                                       start=(part == 0), stop=(part == 1))
                if kind == "tr_qk":
                    mm = turn(step, lambda t: view(qk_sb[:, t, 2 * GJ * n, :], [1, P]), P, rope_ok, b)
                if kind == "maxrow":
                    pe.wait_ge(split_ok, NTH[step])
                    mm = turn(step, lambda t: negmax_p[:, t].rearrange("p a j -> p (a j)"), 2 * GJ)
                if kind == "max":
                    h, t = divmod(n, NT)
                    if t == 0:
                        wait_stacks(pe, b, h)
                        if b == 0:
                            pe.wait_ge(st_bias, h + 1)
                        if maxs == 0:
                            pe.wait_ge(st_const, 16)
                    bank = MAX_BANKS[maxs % len(MAX_BANKS)]
                    wait_max_bank()
                    pe.matmul(ps[bank], q_st[0:ROW_MAX, h, tile(t)], k_st[0:ROW_MAX, h, :],
                              start=True, stop=True).then_inc(max_filled, 1)
                    maxs += 1
                if kind == "exp":
                    t, h = n % PER // GJ, n // PER * GJ + n % GJ
                    if n % PER == 0:
                        pe.wait_ge(st_max[h // GJ], 32 * (b + 1))
                    bank = EXP_BANKS[exps % len(EXP_BANKS)]
                    if exps >= len(EXP_BANKS):
                        pe.wait_ge(exp_ok, exps + 1 - len(EXP_BANKS))
                    elif GIVEN[bank]:
                        wait_read(pe, GIVEN[bank])
                    pe.matmul(ps[bank], k_st[0:ROWS, h, tile(t)], q_st[0:ROWS, h, :],
                              start=True, stop=True).then_inc(exp_filled, 1)
                    exps += 1
                if kind == "pv":
                    t, j = divmod(n % PER, GJ)
                    i = NH * NT * b + n
                    if n % PER == 0:
                        pe.wait_ge(proj_ok, (NT + 2) * (b + 1))
                    if j == 0:
                        pe.wait_ge(exp_ok, i + GJ)
                    mm = pe.matmul(w[VW * j:VW * (j + 1), :], v_sb[:, b, t, n // PER * GJ + j, :], probs[:, i % NPROB, :],
                                   start=(t == 0), stop=(t == NT - 1), tile_position=(0, VW * j))
                if kind == "tr_o":
                    pe.wait_ge(o_ok, NTH[step])
                    mm = turn(step, lambda t: o_sb[:, tile(t)], P)
                if kind == "tr_attn":
                    if n == 0:
                        pe.wait_ge(attn_ok, NG * (b + 1))
                    lo, hi = ((0, KA), (KA, D))[n]
                    mm = turn(step, lambda t: attn[:, t, lo:hi], hi - lo)
                if kind == "out":
                    if n == 0:
                        pe.wait_ge(at_ok, 2 * (b + 1))
                    for k in range(2):
                        pe.matmul(w[:, D * k:D * (k + 1)], at_a[:, tile(2 * n + k)], wa_sb[:, 3 * D:4 * D],
                                  start=True, stop=False)
                        mm = pe.matmul(w[:, D * k:D * (k + 1)], at_b[:, tile(2 * n + k)], wb_sb[0:KB, 3 * D:4 * D],
                                       start=False, stop=True)
                if kind == "up":
                    if n == 0:
                        pe.wait_ge(n3l_ok, 2 * (b + 1))
                        pe.wait_ge(wl_ok[1], 2)
                    lo = 3 * D + P * n
                    pairs = ((0, 0), (1, 0), (0, 1), (2, 2), (3, 2))
                    for k, (i, j) in enumerate(pairs):
                        mm = pe.matmul(w, weights(lo, lo + P)(i), n3[j][:], start=(k == 0), stop=(k == len(pairs) - 1))
                if kind == "down":
                    pe.wait_ge(w2_in, 16)
                    for k in range(2):
                        for f in range(NF):
                            if n == 0 and k == 0:
                                pe.wait_ge(hid_ok, NF * b + f + 1)
                            mm = pe.matmul(w[:, D * k:D * (k + 1)], hid_sb[:, b, f, tile(2 * n + k)], w2_sb[:, f, :],
                                           start=(f == 0), stop=(f == NF - 1))
                if kind == "pv" and n % PER < PER - 1:
                    mm.then_inc(pv_used, 1)
                elif kind in FILLING:
                    mm.then_inc(filled[BANK[step]], 1)

        @block.vector
        def _(dve):
            links = [0]

            def link(ins):
                links[0] += 1
                ins.then_inc(dve_chain, 1)
                dve.wait_ge(dve_chain, links[0])

            def sum_groups(src, ready):
                for k in range(2):
                    dve.wait_ge(*ready[k])
                    dve.tensor_reduce(sums[:, k], view(src[:, 2 * k], [GW, GROUPS], [D, 2], [1, GW]), AX.XY, ALU.add)\
                       .then_inc(summed, 1)

            def stats(src, t):
                dve.bn_stats(stat[:, t, :], src[:, t, :]).then_inc(dve_chain, 1)
                links[0] += 1
                if t == NT - 1:
                    dve.wait_ge(dve_chain, links[0])
                    for k in range(NT):
                        dve.bn_aggr(mv[:, k, :], stat[:, k, :])\
                           .then_inc(*((stats_ok, 1) if k == NT - 1 else (dve_chain, 1)))
                    links[0] += NT - 1

            def normed(src, t, count):
                dve.wait_ge(rstd_ok, count)
                dve.tensor_scalar(z_sb[:, t, :], src[:, t, :], mv[:, t, 0:1], rstd[:, t:t + 1],
                                  ALU.subtract, ALU.mult).then_inc(z_ok, 1)

            def coefficients():
                dve.wait_ge(small_in, 16)
                r = slice(ROW_BIAS, ROW_MAX)
                link(dve.tensor_scalar(coef[r, 0, :], col("ab0", r), col("ca", r), None, ALU.mult))
                link(dve.scalar_tensor_tensor(out=coef[r, 1, :], in0=col("ab1", r), scalar=col("cb", r),
                                              in1=coef[r, 0, :], op0=ALU.mult, op1=ALU.add))
                link(dve.tensor_copy(coef[r, 2, :].bitcast(fp32r), coef[r, 1, :]))
                link(dve.tensor_scalar(coef[r, 0, :], coef[r, 2, :], col("low", r), None, ALU.mult))
                dve.tensor_tensor(coef[r, 3, :], coef[r, 1, :], coef[r, 0, :], ALU.subtract).then_inc(coef_ok, 1)

            maxs = 0
            for step in order("dve"):
                kind, b, n = step
                if kind == "sum" and n == 0:
                    if b:
                        wait_filled(dve, ("gn", 0, 1))
                    sum_groups(x_sb[:, b], [(x_in[2 if b else k], 16) for k in range(2)])
                if kind == "centre":
                    wait_filled(dve, ("gn", b, 0))
                    for k in range(2):
                        dve.tensor_tensor(y_sb[:, b, 2 * k:2 * k + 2],
                                          view(x_sb[:, b, 2 * k], [D, 2], [GW, GROUPS], [1, GW]),
                                          view(work(("gn", b, 0)), [0, 2], [1, GROUPS], [0, GW]), ALU.subtract)\
                           .then_inc(centred, 1)
                if kind == "sum" and n == 1:
                    wait_filled(dve, ("gn", b, 0))
                    sum_groups(squares[:], [(squared, 2 * b + k + 1) for k in range(2)])
                if kind == "var":
                    var_step = ("gn", b, 1)
                    wait_filled(dve, var_step)
                    if b:
                        dve.tensor_copy(stat_g[:, 0, :], work(var_step)[:, 0:GROUPS]).then_inc(vars_ok, 1)
                    else:
                        v, t, r = newton[:, 0, :], newton[:, 1, :], stat_g[:, 1, :]
                        dve.tensor_scalar(v, work(var_step)[:, 0:GROUPS], EPS, None, ALU.add).then_inc(vars_ok, 1)
                        dve.wait_ge(std_ok, 2)
                        link(dve.reciprocal(r, sq[:]))
                        link(dve.tensor_tensor(t, r, r, ALU.mult))
                        dve.wait_ge(vars_ok, 1)
                        link(dve.scalar_tensor_tensor(out=t, in0=t, scalar=-0.5, in1=v, op0=ALU.mult, op1=ALU.mult))
                        link(dve.scalar_tensor_tensor(out=r, in0=t, scalar=1.5, in1=r, op0=ALU.add, op1=ALU.mult))
                if step == ("scale", 0, 0):
                    scale(dve, b)
                if kind == "stats1":
                    dve.wait_ge(gn_ok, b + 1)
                    stats(y_sb[:, b], n)
                if kind == "wbias":
                    wait_filled(dve, step)
                if kind == "wbias" and n == 0:
                    dve.wait_ge(rows_in, 16)
                    half_rows = rows_sb[0:64, 0:DQK]
                    dve.tensor_tensor(half_rows, half_rows, work(step)[0:64, 0:DQK], ALU.add).then_inc(wbias_ok, 1)
                    dve.wait_ge(wbias_ok, 1)
                    link(dve.tensor_copy(bias_p[:], half_rows))
                    dve.tensor_tensor(bias_p[32:64, :], rows_sb[32:64, 0:DQK], bias_p[32:64, :].bitcast(fp32),
                                      ALU.subtract).then_inc(bias_ok, 1)
                    coefficients()
                if kind == "wbias" and n == 1:
                    link(dve.tensor_tensor(bv_sb[:, 0:1], col("bv")[:, 0:1], work(step)[:, 0:1], ALU.add))
                    dve.tensor_tensor(bv_sb[0:KB, 1:2], col("bv", slice(0, KB))[:, 1:2], work(step)[0:KB, 1:2], ALU.add)\
                       .then_inc(wbias_ok, 1)
                if kind == "wbias" and n == 2:
                    dve.tensor_tensor(b1_sb[:], col("b1"), work(step)[:, 0:NF], ALU.add).then_inc(wbias_ok, 1)
                if kind == "wbias" and n == 3:
                    dve.tensor_tensor(rows_sb[:, DQK:3 * D], rows_sb[:, DQK:3 * D], work(step)[:, 0:D], ALU.add)\
                       .then_inc(wbias_ok, 1)
                if kind in ("low1", "low3"):
                    full = work((kind.replace("low", "norm"), b, n))
                    dve.wait_ge(n1h_ok if kind == "low1" else n3h_ok, 2 * b + n + 1)
                    dst = n1 if kind == "low1" else n3
                    if n == 0:
                        ins = dve.tensor_tensor(dst[1][:], full, dst[0][:].bitcast(fp32), ALU.subtract)
                    else:
                        ins = dve.tensor_tensor(dst[2][KB:P, :], full[0:KB, :], dst[2][0:KB, :].bitcast(fp32),
                                                ALU.subtract)
                    ins.then_inc(n1l_ok if kind == "low1" else n3l_ok, 1)
                if kind == "z1" and b == 0:
                    normed(y_sb[:, b], n, 1)
                if kind == "stats3":
                    dve.wait_ge(flat_ok, 2 * b + 2)
                    stats(flat, n)
                if kind == "z3":
                    wait_filled(dve, ("norm1", 1, 1) if b == 0 else ("norm3", 0, 1))
                    normed(flat, n, 4 + b)
                if kind == "direct":
                    wait_filled(dve, step)
                    if n == 0:
                        dve.wait_ge(table_in, 16)
                    dve.tensor_tensor((turned, turned2)[n], work(step), (cos_t, sin_t)[n], ALU.mult)\
                       .then_inc(direct_ok, 1)
                    if n == 1:
                        dve.wait_ge(direct_ok, 2)
                        dve.tensor_tensor(turned, turned, turned2, ALU.add).then_inc(direct_ok, 1)
                if kind == "parts":
                    dve.wait_ge(h_ok, 1)
                    dve.scalar_tensor_tensor(out=qk_l[:, 0, :], in0=turned, scalar=col("qscale"),
                                             in1=qk_h[:, 0, :].bitcast(fp32), op0=ALU.mult, op1=ALU.subtract)\
                       .then_inc(l_ok, 1)
                if kind == "proj" and (b, n) in ROPES[0]:
                    rope(dve, 0, b, n)
                if kind == "tr_qk":
                    dve.wait_ge(h_ok, NG * b + n + 1)
                    if b and n:
                        dve.wait_ge(scr_ok[n], WRITES)
                    elif b:
                        wait_filled(dve, ("stack", 0, 2 * GJ - 1))
                    dve.scalar_tensor_tensor(out=qk_l[:, n, :], in0=work(step), scalar=col("qscale"),
                                             in1=qk_h[:, n, :].bitcast(fp32), op0=ALU.mult, op1=ALU.subtract)\
                       .then_inc(l_ok, 1)
                if kind == "max":
                    h, t = divmod(n, NT)
                    if n % (GJ * NT) == 0 and maxs:
                        dve.wait_ge(split_ok, NG * b + h // GJ)
                    maxs += 1
                    dve.wait_ge(max_filled, maxs)
                    dve.tensor_reduce(negmax[:, t, h % GJ:h % GJ + 1], ps[MAX_BANKS[(maxs - 1) % len(MAX_BANKS)]], AX.X, ALU.max,
                                      negate=True).then_inc(max_ok, 1)
                if kind == "split":
                    dve.wait_ge(max_ok, maxs)
                    if NTH[step] > 1:
                        wait_filled(dve, ("maxrow", *GROUP_LIST[NTH[step] - 2]))
                    link(dve.tensor_copy(negmax_p[:, :, 0, :].bitcast(fp32r), negmax[:]))
                    dve.tensor_tensor(negmax_p[:, :, 1, :], negmax[:], negmax_p[:, :, 0, :], ALU.subtract)\
                       .then_inc(split_ok, 1)
                if kind == "tr_o":
                    wait_filled(dve, step)
                    if n == 0:
                        wait_filled(dve, ("tr_attn", 0, 1) if b else ("tr_qk", 1, NG - 1))
                    if NTH[step] > 1:
                        dve.wait_ge(attn_ok, NTH[step] - 1)
                    link(dve.reciprocal(rec[:], view(work(step)[:, HD:HD + 1], [P, NT], [VW, GJ])))
                    dve.tensor_tensor(view(attn[:, :, 64 * n:64 * (n + 1)], [D, NT], [HD, GJ], [1, HD]),
                                      view(work(step), [P, NT], [VW, GJ], [1, HD]),
                                      view(rec[:], [GJ, NT], [1, GJ], [0, HD]), ALU.mult).then_inc(attn_ok, 1)
                if kind == "out":
                    wait_filled(dve, step)
                    dve.wait_ge(ybo_ok, b + 1)
                    if b and n == 0:
                        dve.wait_ge(res_ok, b)
                    dve.tensor_tensor(flat[:, 2 * n:2 * n + 2, :], view(work(step), [D, 2], [1, D]),
                                      y_sb[:, b, 2 * n:2 * n + 2, :], ALU.add).then_inc(flat_ok, 1)
                if kind == "down":
                    wait_filled(dve, step)
                    dve.wait_ge(res_ok, b + 1)
                    if b:
                        dve.wait_ge(stored, 16 * 2 * b)
                    dve.tensor_tensor(y_out[:, 2 * n:2 * n + 2, :], view(work(step), [D, 2], [1, D]),
                                      x_sb[:, b, 2 * n:2 * n + 2, :], ALU.add).then_inc(out_ok, 1)


def kernel(**inputs):
    import numpy as np
    import concourse.bacc as bacc
    from concourse.bass_utils import run_bass_kernel_spmd as run

    p = {k.removeprefix("L0_conv_"): np.asarray(v) for k, v in inputs.items()}
    f = np.float32

    def chunks(v):
        a = np.zeros((P, 2), f)
        a[:, 0] = v[:KA]
        a[:, 1] = np.tile(v[KA:], 2)
        return a

    fraction = f(2.0) * np.arange(4, dtype=f) / f(HD)
    angles = np.arange(T, dtype=f)[:, None] / (f(10000.0) ** fraction).astype(f)[None, :]
    table = {"cos": np.cos(angles), "sin": np.sin(angles), "nsin": -np.sin(angles)}
    table = {k: v.astype(f).reshape(NT, P, 4).transpose(1, 0, 2).reshape(P, NT * 4) for k, v in table.items()}
    row = np.arange(P)
    low = ((row >= ROW_BIAS + C) & (row < ROW_BIAS + 2 * C)) | (row == ROW_BIAS + 2 * C + 1)
    is_b1 = row >= ROW_BIAS + 2 * C
    small = np.concatenate([
        np.eye(P, dtype=f), table["cos"], table["sin"], table["nsin"], chunks(p["ln1_g"]), chunks(p["ln1_b"]),
        chunks(p["ln3_g"]), chunks(p["ln3_b"]), p["b1"].reshape(NF, P).T, chunks(p["bv"]),
        np.where(row < GJ * HD, f(HD ** -0.5), f(1))[:, None], low.astype(f)[:, None],
        np.where(is_b1, 0, 1).astype(f)[:, None], np.where(is_b1, 1, -1).astype(f)[:, None],
        np.broadcast_to(p["attn_biases"][:, 0], (P, NH)), np.broadcast_to(p["attn_biases"][:, 1], (P, NH))], axis=1)

    def turns(q, k):
        both = np.stack([a.reshape(-1, NG, GJ * HD) for a in (q, k)], axis=2)
        return both.reshape(*q.shape[:-1], 2 * D)

    w = np.concatenate([turns(p["wq"], p["wk"]), p["wv"], p["wo"], p["w1"]], axis=1)
    onehot = (np.arange(C)[:, None] == np.arange(T)[None, :] // S).astype(f)
    arrays = {
        "x": p["x"], "small": small, "wa": w[:KA], "wb": w[KA:],
        "w2": p["w2"].reshape(NF, P, D).transpose(1, 0, 2),
        "rows": np.concatenate([turns(p["bq"], p["bk"]), p["bo"], p["b2"]]),
        "keyrows": np.concatenate([onehot, onehot, np.ones((ROWS - ROW_BIAS - 2 * C, T), f)]),
    }
    dim = np.arange(P) % HD
    cos_t, sin_t = np.ones((P, T), f), np.zeros((P, T), f)
    for at, sign in ((0, -1), (HD // 2, 1)):
        for k in range(4):
            cos_t[dim == at + k] = np.cos(angles[:, k]).astype(f)
            sin_t[dim == at + k] = (sign * np.sin(angles[:, k])).astype(f)
    arrays["table"] = np.concatenate([cos_t, sin_t], axis=1)
    nc = bacc.Bacc("TRN2", target_bir_lowering=False, num_devices=1)
    arrays = {f"in_{k}": np.ascontiguousarray(v) for k, v in arrays.items()}
    args = [nc.dram_tensor(k, v.shape, fp32, kind="ExternalInput").ap() for k, v in arrays.items()]
    out = nc.dram_tensor("out_0", (B, C, S, D), fp32, kind="ExternalOutput").ap()
    build(nc, *args, out)
    return run(nc, [arrays], core_ids=[0]).results[0]["out_0"]
```
